# Optimizing a Trainium2 kernel written in Bass

```python
import numpy as np
import jax
import jax.numpy as jnp

def _softmax(x, axis=-1):
    return jax.nn.softmax(x, axis=axis)
def _gelu(x):
    return jax.nn.gelu(x, approximate=True)
def _silu(x):
    return jax.nn.silu(x)
def _sigmoid(x):
    return jax.nn.sigmoid(x)
def _layernorm(x, axis=-1, eps=1e-5):
    m = jnp.mean(x, axis=axis, keepdims=True)
    v = jnp.var(x, axis=axis, keepdims=True)
    return (x - m) / jnp.sqrt(v + eps)
def _scatter_add(tgt, idx, src, axis=0):
    return tgt.at[idx].add(src)
def _segment_sum(src, seg, n):
    return jax.ops.segment_sum(src, seg, n)

kernel_name = 'mk_conv_preact_d1_conv_nchw256_988218'

def setup_inputs(seed: int = 0):
    np.random.seed(seed)
    _w = jnp.asarray
    def _rec_inputs():
        import jax
        import jax.numpy as jnp
        _gk = jax.random.key(seed)
        x = -0.000125 + 0.9999 * jax.random.normal(jax.random.fold_in(_gk, 1), (8, 256, 128, 128), jnp.float32)
        return x
    x = _rec_inputs()
    def _L0_conv_setup():
        import jax, jax.numpy as jnp
        import numpy as np
        B, C, H, W = (8, 256, 128, 128)
        HEADS = 16
        HEADC = C // HEADS
        EPS = 1e-05

        def _layernorm(x, w, b):
            mean = jnp.mean(x, axis=-1, keepdims=True)
            std = jnp.std(x, axis=-1, keepdims=True, ddof=1)
            return (x - mean) / (std + EPS) * w + b
        key = jax.random.key(seed)
        k1, k2 = jax.random.split(key)
        x = jax.random.normal(k1, (B, C, H, W), dtype=jnp.float32)
        w_qkv = jax.random.normal(k2, (3 * C, C), dtype=jnp.float32) * (1.0 / np.sqrt(C))
        b_qkv = jnp.zeros((3 * C,), dtype=jnp.float32)
        kln_w = jnp.ones((HEADS, HEADC), dtype=jnp.float32)
        kln_b = jnp.zeros((HEADS, HEADC), dtype=jnp.float32)
        vln_w = jnp.ones((HEADS, HEADC), dtype=jnp.float32)
        vln_b = jnp.zeros((HEADS, HEADC), dtype=jnp.float32)
        return {'x': x, 'w_qkv': w_qkv, 'b_qkv': b_qkv, 'kln_w': kln_w, 'kln_b': kln_b, 'vln_w': vln_w, 'vln_b': vln_b}
    _L0_conv_all = _L0_conv_setup()
    _L0_conv_in = {k: v for k, v in _L0_conv_all.items() if k in ('w_qkv', 'b_qkv', 'kln_w', 'kln_b', 'vln_w', 'vln_b', )}
    del _L0_conv_all

    return {
        "x": x,
        "L0_conv_w_qkv": _L0_conv_in["w_qkv"],
        "L0_conv_b_qkv": _L0_conv_in["b_qkv"],
        "L0_conv_kln_w": _L0_conv_in["kln_w"],
        "L0_conv_kln_b": _L0_conv_in["kln_b"],
        "L0_conv_vln_w": _L0_conv_in["vln_w"],
        "L0_conv_vln_b": _L0_conv_in["vln_b"],
    }

def reference(x, L0_conv_w_qkv, L0_conv_b_qkv, L0_conv_kln_w, L0_conv_kln_b, L0_conv_vln_w, L0_conv_vln_b):
    import jax
    import jax.numpy as jnp
    def _L0_conv_ref(x, w_qkv, b_qkv, kln_w, kln_b, vln_w, vln_b):
        import jax, jax.numpy as jnp
        import numpy as np
        B, C, H, W = (8, 256, 128, 128)
        HEADS = 16
        HEADC = C // HEADS
        EPS = 1e-05

        def _layernorm(x, w, b):
            mean = jnp.mean(x, axis=-1, keepdims=True)
            std = jnp.std(x, axis=-1, keepdims=True, ddof=1)
            return (x - mean) / (std + EPS) * w + b
        b, c, h, w = x.shape
        n = h * w
        qkv = jnp.einsum('bchw,oc->bhwo', x, w_qkv) + b_qkv
        qkv = qkv.reshape(b, n, HEADS, -1)
        q, k, v = jnp.split(qkv, 3, axis=-1)
        k = _layernorm(k, kln_w, kln_b)
        v = _layernorm(v, vln_w, vln_b)
        kv = jnp.einsum('bnhd,bnhe->bhde', k, v) / n
        out = jnp.einsum('bnhd,bhde->bnhe', q, kv)
        out = out.reshape(b, h, w, c).transpose(0, 3, 1, 2)
        return out

    def _gn(v, G=32, eps=1e-5):
        B_, C_, H_, W_ = v.shape
        g = v.reshape(B_, G, C_ // G, H_, W_)
        m = jnp.mean(g, axis=(2, 3, 4), keepdims=True)
        s = jnp.var(g, axis=(2, 3, 4), keepdims=True)
        return ((g - m) / jnp.sqrt(s + eps)).reshape(v.shape)

    def _ln_c(v, eps=1e-6):
        m = jnp.mean(v, axis=1, keepdims=True)
        s = jnp.var(v, axis=1, keepdims=True)
        return (v - m) / jnp.sqrt(s + eps)

    def _ln_t(v, eps=1e-5):
        m = jnp.mean(v, axis=-1, keepdims=True)
        s = jnp.var(v, axis=-1, keepdims=True)
        return (v - m) / jnp.sqrt(s + eps)

    def _to_tokens(v):
        B_, C_, H_, W_ = v.shape
        return v.reshape(B_, C_, H_ * W_).transpose(0, 2, 1)
    def _from_tokens(t, like):
        B_, C_, H_, W_ = like.shape
        return t.transpose(0, 2, 1).reshape(B_, C_, H_, W_)

    x = x + _L0_conv_ref(_gn(x), L0_conv_w_qkv, L0_conv_b_qkv, L0_conv_kln_w, L0_conv_kln_b, L0_conv_vln_w, L0_conv_vln_b)
    return x


_drawn_inputs = setup_inputs


def setup_inputs(seed=0):
    import zlib

    import numpy as np

    out = dict(_drawn_inputs(seed))
    spreads = {'L0_conv_b_qkv': (0.0, 0.1),
     'L0_conv_kln_w': (1.0, 0.2),
     'L0_conv_kln_b': (0.0, 0.1),
     'L0_conv_vln_w': (1.0, 0.2),
     'L0_conv_vln_b': (0.0, 0.1)}
    factors = {}
    for name, (base, spread) in spreads.items():
        noise = np.random.default_rng([zlib.crc32(name.encode()), seed]).standard_normal(out[name].shape)
        drawn = base * np.exp(spread * noise) if base else spread * noise
        out[name] = jnp.asarray(drawn.astype(out[name].dtype))
    for name, factor in factors.items():
        out[name] = (out[name] * factor).astype(out[name].dtype)
    return out
```

```python
from contextlib import ExitStack

import concourse.bass as bass
from concourse import mybir

B, C, H, W = 8, 256, 128, 128
N = H * W
HEADS, D = 16, 16
J = D - 1
P = 128
HALVES = C // P
NG = 32
GROUP = C // NG
PAIR = 2 * 3 * D
PAIRS = HEADS // 2
GN_EPS, LN_EPS = 1e-5, 1e-5

BLOCK = 2048
BLOCKS = N // BLOCK
SLOTS = BLOCKS + 1
QTOK = 512
QUARTERS = BLOCK // QTOK
TILE = 128
GT = 2
STEPS = BLOCK // (TILE * GT)
SPQ = STEPS // QUARTERS
ISTEPS = STEPS * BLOCKS
KV = 2 * HEADS * J
UNITS = 4
UTOK = BLOCK // 2
IMAGE_OWN = 6
GRANT = 2
Y_SCALE = 64.0
W_SCALE = 1024.0

C_HEL, C_QG, C_EG = 0, 60, 92
C_QL, C_EL, C_MASK, C_AVG, C_E3 = 124, 252, 380, 508, 636
C_WIDTH = 640

fp32 = mybir.dt.float32
fp16 = mybir.dt.float16
bf16 = mybir.dt.bfloat16
ALU = mybir.AluOpType
ACT = mybir.ActivationFunctionType
AX = mybir.AxisListType
RMAX = bass.bass_isa.ReduceOp.max


def build(nc, x, w_qkv, b_qkv, kln_w, kln_b, vln_w, vln_b, consts, out):
    x_v = x.rearrange("b (a p) h w -> b p a (h w)", p=P)
    out_v = out.rearrange("b (a p) h w -> b p a (h w)", p=P)

    ctx = ExitStack()
    with ctx:
        def sb(name, shape, dt):
            return ctx.enter_context(nc.sbuf_tensor(name, shape, dt))

        def sem(name):
            return ctx.enter_context(nc.semaphore(name))

        ring = sb("ring", [P, SLOTS, HALVES, BLOCK], fp32)
        y_hi = sb("y_hi", [P, QUARTERS, HALVES, QTOK], fp16)
        y_lo = sb("y_lo", [P, QUARTERS, HALVES, QTOK], fp16)
        kv = sb("kv", [P, 4, GT, 2 * HEADS, D], fp32)
        scratch = sb("scratch", [P, 2, UTOK], fp32)
        ssq = sb("ssq", [P, 4, GT, 2 * HEADS], fp32)
        sigma = sb("sigma", [P, 4, GT, 2 * HEADS], fp32)
        sig_kv = sb("sig_kv", [P, 4, GT, HEADS], fp32)
        inv_kv = sb("inv_kv", [P, 4, GT, HEADS], fp32)
        w_hi = sb("w_hi", [P, HALVES, KV], fp16)
        w_lo = sb("w_lo", [P, HALVES, KV], fp16)
        bias_rows = sb("bias_rows", [P, KV], bf16)
        ones_rows = sb("ones_rows", [P, P], bf16)
        eps_h = sb("eps_h", [P, 2 * HEADS], fp32)
        tab = sb("tab", [P, C_WIDTH], fp32)
        g_mat = sb("g_mat", [P, 2, C + 1], fp32)
        l_mat = sb("l_mat", [P, 2, P], fp32)
        s_mat = sb("s_mat", [P, 2, P], fp32)
        u_mat = sb("u_mat", [P, 2, C + 1], fp32)
        m_mat = sb("m_mat", [P, HALVES, C], fp32)
        shift = sb("shift", [P, HALVES], fp32)
        stats = sb("stats", [P, HALVES, N // 512, 6], fp32)
        chan = sb("chan", [P, HALVES, 2], fp32)
        dev = sb("dev", [P, HALVES], fp32)
        dev2 = sb("dev2", [P, HALVES], fp32)
        gmean = sb("gmean", [P, HALVES], fp32)
        gvar = sb("gvar", [P, HALVES], fp32)
        std = sb("std", [P, HALVES], fp32)
        rstd = sb("rstd", [P, HALVES], fp32)
        y_scale = sb("y_scale", [P, HALVES], fp32)
        x_scale = sb("x_scale", [P, HALVES], fp32)

        room = ring[:, SLOTS - 1, :, :].rearrange("p a n -> p (a n)")
        at = [0]

        def setup_room(rows, width):
            at[0] += width
            assert at[0] <= HALVES * BLOCK
            return room[0:rows, at[0] - width:at[0]]

        wt = setup_room(PAIR, PAIRS * (C + 1)).rearrange("p (t n) -> p t n", t=PAIRS)
        b3 = setup_room(PAIR, PAIRS * 3).rearrange("p (t n) -> p t n", t=PAIRS)
        klw = setup_room(PAIR, PAIRS)
        klb = setup_room(PAIR, PAIRS)
        lk = setup_room(PAIR, PAIRS * 32).rearrange("p (t n) -> p t n", t=PAIRS)
        vlw = setup_room(P, C)
        vlb = setup_room(P, C)
        wmax = setup_room(P, HALVES * 32).rearrange("p (a n) -> p a n", a=HALVES)
        bmax = setup_room(3, 32)
        amax = setup_room(P, 32)
        alpha = setup_room(P, 32)
        ws = room[:, 0:KV]
        bs = room[0:3, KV:2 * KV]
        bpart = room[0:3, 2 * KV:3 * KV]

        prod = ctx.enter_context(nc.psum_tensor("prod", [P, 4, 512], fp32))
        acc = ctx.enter_context(nc.psum_tensor("acc", [P, 2, 512], fp32))
        small = ctx.enter_context(nc.psum_tensor("small", [P, 512], fp32))

        hel = tab[0:PAIR, C_HEL:C_HEL + 60].rearrange("p (v x) -> p v x", v=2)
        avg = tab[:, C_AVG:C_AVG + P]
        mask = tab[:, C_MASK:C_MASK + P]

        consts_in = sem("consts_in")
        setup_cleared = sem("setup_cleared")
        setup_w = sem("setup_w")
        setup_g = sem("setup_g")
        setup_lk = sem("setup_lk")
        setup_amax = sem("setup_amax")
        setup_wmax = sem("setup_wmax")
        setup_b3 = sem("setup_b3")
        setup_done = sem("setup_done")
        first_in = [sem(f"first_in{i}") for i in range(BLOCKS)]
        refill_in = sem("refill_in")
        stored = sem("stored")
        chan_ready = sem("chan_ready")
        group_sum = sem("group_sum")
        var_ready = sem("var_ready")
        std_ready = sem("std_ready")
        normed = sem("normed")
        hi_ready = sem("hi_ready")
        split_ready = sem("split_ready")
        projected = sem("projected")
        squared = sem("squared")
        copied = sem("copied")
        summed = sem("summed")
        sigma_ready = sem("sigma_ready")
        sig_kv_ready = sem("sig_kv_ready")
        v_scaled = sem("v_scaled")
        kv_done = sem("kv_done")
        s_ready = sem("s_ready")
        u_prod = sem("u_prod")
        u_ready = sem("u_ready")
        m_prod = sem("m_prod")
        m_ready = sem("m_ready")
        mixed = sem("mixed")
        evacuated = sem("evacuated")
        added = sem("added")
        pool_sig = sem("pool_sig")
        act_setup = sem("act_setup")
        inv_ready = sem("inv_ready")
        stats_done = sem("stats_done")
        dve_step = sem("dve_step")

        block = ctx.enter_context(nc.Block())

        def y_block(g):
            return ring[:, bass.ds(g % SLOTS, 1), :, :] if not isinstance(g, int) else \
                ring[:, g % SLOTS:g % SLOTS + 1, :, :]

        def images(eng, body):
            with eng.Fori(0, B - 1) as b:
                body(b, True)
            body(B - 1, False)

        def blocks(eng, body):
            body(0, True, False)
            with eng.Fori(1, BLOCKS - 1) as k:
                body(k, False, False)
            body(BLOCKS - 1, False, True)

        @block.sync
        def _(sp):
            sp.dma_start(tab[:, :], consts).then_inc(consts_in, 16)
            with nc.allow_non_contiguous_dma(reason="small parameters"):
                sp.dma_start(wt[:, :, 0:C], w_qkv.rearrange("(t p) c -> p t c", p=PAIR)).then_inc(consts_in, 16)
                sp.dma_start(wt[:, :, C:C + 1], b_qkv.rearrange("(t p one) -> p t one", p=PAIR, one=1)).then_inc(consts_in, 16)
                sp.dma_start(vlw, vln_w.rearrange("(one h) d -> one (h d)", one=1).to_broadcast([P, C])).then_inc(consts_in, 16)
                sp.dma_start(vlb, vln_b.rearrange("(one h) d -> one (h d)", one=1).to_broadcast([P, C])).then_inc(consts_in, 16)
                sp.wait_ge(setup_cleared, 1)
                for row in range(2):
                    q0 = row * 3 * D
                    sp.dma_start(klw[q0:q0 + D, :], kln_w.rearrange("(t r) d -> r d t", r=2)[row]).then_inc(consts_in, 16)
                    sp.dma_start(klb[q0:q0 + D, :], kln_b.rearrange("(t r) d -> r d t", r=2)[row]).then_inc(consts_in, 16)
            for g in range(BLOCKS):
                if g >= 3:
                    sp.wait_ge(first_in[g - 3], 16)
                sp.dma_start(ring[:, g, :, :], x_v[0, :, :, g * BLOCK:(g + 1) * BLOCK]).then_inc(first_in[g], 16)
            sp.wait_ge(setup_done, 1)
            sp.dma_start(ring[:, SLOTS - 1, :, :], x_v[1, :, :, 0:BLOCK]).then_inc(refill_in, 16)

            def store(b, k, g):
                o = sp.snap(b * (C * N) + k * BLOCK)
                slot = sp.snap((g % SLOTS) * (HALVES * BLOCK))
                sp.wait_ge(added, GRANT + UNITS * (g + 1))
                sp.dma_start(block_at(out, o), slot_at(slot)).then_inc(stored, 16)

            def refill(b, k, g):
                o = sp.snap(b * (C * N) + k * BLOCK)
                slot = sp.snap((g % SLOTS) * (HALVES * BLOCK))
                sp.wait_ge(stored, 16 * (g + 1))
                sp.wait_ge(refill_in, 16 * (g + 1))
                sp.dma_start(slot_at(slot), block_at(x, o)).then_inc(refill_in, 16)

            ring_flat = ring[:, :, :, :].rearrange("p s a n -> p (s a n)")

            def slot_at(slot):
                return ring_flat[:, bass.ds(slot, HALVES * BLOCK)].rearrange("p (a n) -> p a n", a=HALVES)

            def block_at(t, o):
                return bass.AP(tensor=t.tensor, offset=o, ap=[[N, P], [P * N, HALVES], [1, BLOCK]])

            with sp.Fori(0, B - 2) as b:
                with sp.Fori(0, BLOCKS - 1) as k:
                    store(b, k, b * BLOCKS + k)
                    refill(b + 1, k + 1, b * BLOCKS + k)
                store(b, BLOCKS - 1, b * BLOCKS + BLOCKS - 1)
                refill(b + 2, 0, b * BLOCKS + BLOCKS - 1)
            b = B - 2
            with sp.Fori(0, BLOCKS - 1) as k:
                store(b, k, b * BLOCKS + k)
                refill(b + 1, k + 1, b * BLOCKS + k)
            store(b, BLOCKS - 1, b * BLOCKS + BLOCKS - 1)
            b = B - 1
            with sp.Fori(0, BLOCKS) as k:
                store(b, k, b * BLOCKS + k)
            sp.wait_ge(stored, 16 * B * BLOCKS)

        @block.gpsimd
        def _(pool):
            nc.gpsimd.memset(klw, 0.0)
            nc.gpsimd.memset(klb, 0.0).then_inc(setup_cleared, 1)
            pool.wait_ge(setup_wmax, 1)
            nc.gpsimd.partition_all_reduce(amax, wmax[:, 0, :], P, RMAX).then_inc(setup_amax, 1)

            def lows(b, k, q):
                g = b * BLOCKS + k
                pool.wait_ge(hi_ready, QUARTERS * g + q + 1)
                nc.gpsimd.tensor_tensor(
                    y_lo[:, q:q + 1, :, :], y_block(g)[:, :, :, q * QTOK:(q + 1) * QTOK],
                    y_hi[:, q:q + 1, :, :], ALU.subtract).then_inc(split_ready, 1)

            def sigmas(n, j):
                pool.wait_ge(sigma_ready, n + 1)
                s16 = kv[:, j % 4, :, :, J]
                nc.gpsimd.tensor_tensor(s16, sigma[:, j % 4, :, :],
                                        eps_h[:, None, :].to_broadcast([P, GT, 2 * HEADS]),
                                        ALU.add).then_inc(pool_sig, 1)
                pool.wait_ge(pool_sig, n + 1)
                nc.gpsimd.tensor_tensor(sig_kv[:, j % 4, :, :], kv[:, j % 4, :, 0:HEADS, J],
                                        kv[:, j % 4, :, HEADS:, J], ALU.mult).then_inc(sig_kv_ready, 1)

            def image(b, more):
                for q in range(2):
                    lows(b, 0, q)

                def body(k, first, last):
                    n0 = (b * BLOCKS + k) * STEPS
                    for j in range(STEPS):
                        sigmas(n0 + j, j)
                        if j % SPQ == SPQ - 1:
                            q = j // SPQ + 2
                            if q < QUARTERS:
                                lows(b, k, q)
                            elif not last:
                                lows(b, k + 1, q - QUARTERS)
                blocks(pool, body)

            images(pool, image)

        @block.scalar
        def _(act):
            act.wait_ge(setup_g, 1)
            nc.scalar.activation(g_mat[:, 0, :], acc[:, 0, 0:C + 1], ACT.Copy).then_inc(act_setup, 1)
            nc.scalar.activation(g_mat[:, 1, :], acc[:, 1, 0:C + 1], ACT.Copy).then_inc(act_setup, 1)
            act.wait_ge(act_setup, 2)
            nc.scalar.activation(shift[:, :], tab[:, 0:HALVES], ACT.Copy).then_inc(evacuated, GRANT)

            def group_std(b):
                act.wait_ge(var_ready, b + 1)
                nc.scalar.activation(std[:, :], gvar[:, :], ACT.Sqrt).then_inc(std_ready, 1)

            def highs(b, k, q, waits):
                g = b * BLOCKS + k
                act.wait_ge(normed, QUARTERS * g + q + 1)
                if waits:
                    act.wait_ge(projected, SPQ * (QUARTERS * g + q - QUARTERS + 1))
                nc.scalar.activation(y_hi[:, q:q + 1, :, :], y_block(g)[:, :, :, q * QTOK:(q + 1) * QTOK],
                                     ACT.Copy).then_inc(hi_ready, 1)

            def image(b, more):
                for q in range(2):
                    highs(b, 0, q, False)

                def body(k, first, last):
                    n0 = (b * BLOCKS + k) * STEPS
                    for j in range(STEPS):
                        n = n0 + j
                        z = prod[:, 2 * (j % 2):2 * (j % 2) + 2, 0:KV]
                        act.wait_ge(projected, n + 1)
                        if not (first and j < 2):
                            act.wait_ge(summed, n - 1)
                        nc.scalar.activation(
                            scratch[:, j % 2, 0:GT * KV].rearrange("p (t n) -> p t n", t=GT), z,
                            ACT.Square).then_inc(squared, 1)
                        if not (first and j < 4):
                            act.wait_ge(kv_done, n - 3)
                        nc.scalar.activation(
                            kv[:, j % 4, :, :, 0:J],
                            z.rearrange("p t (h j) -> p t h j", j=J), ACT.Copy).then_inc(copied, 1)
                        act.wait_ge(summed, n + 1)
                        nc.scalar.activation(sigma[:, j % 4, :, :], ssq[:, j % 4, :, :], ACT.Sqrt,
                                             scale=1.0 / (D - 1)).then_inc(sigma_ready, 1)
                        if j % SPQ == SPQ - 1:
                            q = j // SPQ + 2
                            if q < QUARTERS:
                                highs(b, k, q, not first)
                            elif not last:
                                highs(b, k + 1, q - QUARTERS, True)
                blocks(act, body)

                act.wait_ge(u_prod, b + 1)
                nc.scalar.activation(u_mat[:, :, :], prod[:, 0:2, 0:C + 1], ACT.Copy).then_inc(u_ready, 1)

                act.wait_ge(m_ready, b + 1)
                with act.Fori(0, BLOCKS) as k:
                    g = b * BLOCKS + k
                    for u in range(UNITS):
                        n = UNITS * g + u
                        half = u % 2
                        act.wait_ge(mixed, n + 1)
                        act.wait_ge(added, n + 1)
                        nc.scalar.activation(
                            scratch[:, u % 2, :].rearrange("p (t n) -> p t n", t=2),
                            prod[:, 2 * (u % 2):2 * (u % 2) + 2, :], ACT.Identity,
                            bias=shift[:, half:half + 1]).then_inc(evacuated, 1)
                if more:
                    group_std(b + 1)

            group_std(0)
            images(act, image)

        @block.vector
        def _(dve):
            count = [0, 0]

            def own(ins):
                count[1] += 1
                ins.then_inc(dve_step, 1)
                dve.wait_ge(dve_step, count[0] + count[1])

            dve.memset(bias_rows[:, :], 0.0)
            dve.memset(ones_rows[:, :], 1.0)
            dve.wait_ge(consts_in, 16 * 9)
            own(dve.tensor_copy(b3, wt[:, :, C:C + 1].to_broadcast([PAIR, PAIRS, 3])))
            qg = tab[0:PAIR, C_QG:C_QG + 32]
            eg = tab[0:PAIR, C_EG:C_EG + 32]
            for t in range(PAIRS):
                own(dve.tensor_scalar(lk[:, t, :], qg, klw[:, t:t + 1], None, ALU.mult))
            for t in range(PAIRS):
                ins = dve.scalar_tensor_tensor(lk[:, t, :], eg, klb[:, t:t + 1], lk[:, t, :], ALU.mult, ALU.add)
            ins.then_inc(setup_lk, 1)
            for g in range(2):
                own(dve.tensor_tensor(l_mat[:, g, :], tab[:, C_QL:C_QL + P], vlw[:, g * P:(g + 1) * P], ALU.mult))
                own(dve.tensor_tensor(vlb[:, g * P:(g + 1) * P], tab[:, C_EL:C_EL + P], vlb[:, g * P:(g + 1) * P], ALU.mult))
                own(dve.tensor_tensor(l_mat[:, g, :], l_mat[:, g, :], vlb[:, g * P:(g + 1) * P], ALU.add))
            dve.wait_ge(setup_w, 1)
            for a in range(HALVES):
                own(dve.tensor_reduce(wmax[:, a, :], prod[:, a, 0:KV].rearrange("p (h j) -> p h j", j=J),
                                      AX.X, ALU.max, apply_absolute_value=True))
            own(dve.tensor_reduce(bmax, prod[0:3, 2, 0:KV].rearrange("p (h j) -> p h j", j=J),
                                  AX.X, ALU.max, apply_absolute_value=True))
            own(dve.tensor_tensor(wmax[:, 0, :], wmax[:, 0, :], wmax[:, 1, :], ALU.max))
            dve.tensor_tensor(wmax[0:3, 0, :], wmax[0:3, 0, :], bmax, ALU.max).then_inc(setup_wmax, 1)
            dve.wait_ge(setup_amax, 1)
            own(dve.tensor_scalar(amax, amax, 1e-30, None, ALU.max))
            own(dve.reciprocal(alpha, amax))
            own(dve.tensor_scalar(eps_h[:, :], alpha, LN_EPS * W_SCALE * Y_SCALE, None, ALU.mult))
            own(dve.tensor_scalar(alpha, alpha, W_SCALE, None, ALU.mult))
            dve.wait_ge(setup_g, 1)
            for a in range(HALVES):
                own(dve.tensor_tensor(ws.rearrange("p (h j) -> p h j", j=J),
                                      prod[:, a, 0:KV].rearrange("p (h j) -> p h j", j=J),
                                      alpha[:, :, None].to_broadcast([P, 2 * HEADS, J]), ALU.mult))
                own(dve.tensor_copy(w_hi[:, a, :], ws))
                own(dve.tensor_tensor(w_lo[:, a, :], ws, w_hi[:, a, :], ALU.subtract))
            own(dve.tensor_tensor(bs.rearrange("p (h j) -> p h j", j=J),
                                  prod[0:3, 2, 0:KV].rearrange("p (h j) -> p h j", j=J),
                                  alpha[0:3, :, None].to_broadcast([3, 2 * HEADS, J]), ALU.mult))
            own(dve.tensor_scalar(bs, bs, Y_SCALE, None, ALU.mult))
            below = tab[0:3, C_E3:C_E3 + 3]
            for i in range(3):
                own(dve.tensor_copy(bias_rows[0:3, :], bs))
                if i < 2:
                    own(dve.tensor_scalar(bpart, bias_rows[0:3, :], below[:, i:i + 1], None, ALU.mult))
                    own(dve.tensor_tensor(bs, bs, bpart, ALU.subtract))
            dve.tensor_copy(gmean[:, :], tab[:, 0:HALVES]).then_inc(added, GRANT)
            dve.tensor_copy(gvar[:, :], tab[:, 0:HALVES]).then_inc(setup_done, 1)

            def block_stats(g, k, parts):
                src = y_block(g)
                for p in parts:
                    a, s = p % 2, p // 2
                    if isinstance(k, int):
                        o = stats[:, a, k * 4 + s, :]
                    else:
                        o = stats[:, a, bass.ds(k * 4 + s, 1), :]
                    dve.bn_stats(o, src[:, 0, a, s * 512:(s + 1) * 512] if isinstance(g, int)
                                 else src[:, :, a, s * 512:(s + 1) * 512]).then_inc(stats_done, 1)

            def finish_stats(b):
                dve.wait_ge(stats_done, 64 * (b + 1))
                dve.memset(dev[:, :], 0.0)
                for a in range(HALVES):
                    ins = dve.bn_aggr(chan[:, a, :], stats[:, a, :, :])
                ins.then_inc(chan_ready, 1)
                dve.wait_ge(group_sum, 2 * b + 1)
                own(dve.tensor_copy(gmean[:, :], small[:, 0:HALVES]))
                own(dve.tensor_tensor(dev[:, :], chan[:, :, 0], gmean[:, :], ALU.subtract))
                own(dve.tensor_tensor(dev2[:, :], dev[:, :], dev[:, :], ALU.mult))
                dve.tensor_tensor(dev[:, :], dev2[:, :], chan[:, :, 1], ALU.add).then_inc(chan_ready, 1)
                dve.wait_ge(group_sum, 2 * b + 2)
                dve.tensor_scalar(gvar[:, :], small[:, 0:HALVES], GN_EPS, None, ALU.add).then_inc(var_ready, 1)
                dve.wait_ge(std_ready, b + 1)
                own(dve.reciprocal(rstd[:, :], std[:, :]))
                own(dve.tensor_scalar(y_scale[:, :], rstd[:, :], Y_SCALE, None, ALU.mult))
                own(dve.tensor_scalar(x_scale[:, :], std[:, :], 1.0 / Y_SCALE, None, ALU.mult))

            def normalise(b, k, q):
                g = b * BLOCKS + k
                src = y_block(g)
                for a in range(HALVES):
                    v = src[:, :, a, q * QTOK:(q + 1) * QTOK]
                    ins = dve.tensor_scalar(v, v, gmean[:, a:a + 1], y_scale[:, a:a + 1],
                                            ALU.subtract, ALU.mult)
                ins.then_inc(normed, 1)

            def sum_squares(n, j):
                dve.wait_ge(squared, n + 1)
                dve.tensor_reduce(ssq[:, j % 4, :, :],
                                  scratch[:, j % 2, 0:GT * KV].rearrange("p (t h j) -> p t h j", t=GT, j=J),
                                  AX.X, ALU.add).then_inc(summed, 1)

            def scale_v(n, j):
                dve.wait_ge(sig_kv_ready, n + 1)
                dve.reciprocal(kv[:, j % 4, :, HEADS:, J], kv[:, j % 4, :, 0:HEADS, J])
                dve.reciprocal(inv_kv[:, j % 4, :, :], sig_kv[:, j % 4, :, :]).then_inc(inv_ready, 1)
                dve.wait_ge(copied, n + 1)
                dve.wait_ge(inv_ready, n + 1)
                for t in range(GT):
                    v = kv[:, j % 4, t, HEADS:, 0:J]
                    ins = dve.tensor_tensor(v, v, inv_kv[:, j % 4, t, :, None].to_broadcast([P, HEADS, J]), ALU.mult)
                ins.then_inc(v_scaled, 1)

            for k in range(BLOCKS):
                dve.wait_ge(first_in[k], 16)
                block_stats(k, k, range(8))
            finish_stats(0)
            setup_steps = count[1]

            def image(b, more):
                count[0], count[1] = b * IMAGE_OWN + setup_steps, 0
                for q in range(3):
                    normalise(b, 0, q)

                def body(k, first, last):
                    n0 = (b * BLOCKS + k) * STEPS
                    for j in range(STEPS):
                        sum_squares(n0 + j, j)
                        if j == 0:
                            normalise(b, k, 3)
                        elif j % SPQ == 0 and not last:
                            normalise(b, k + 1, j // SPQ - 1)
                        if not (first and j == 0):
                            scale_v(n0 + j - 1, (j - 1) % STEPS)
                    if last:
                        scale_v(n0 + STEPS - 1, STEPS - 1)
                blocks(dve, body)

                dve.wait_ge(kv_done, ISTEPS * (b + 1))
                dve.tensor_tensor(s_mat[:, :, :], acc[:, :, 0:P],
                                  mask[:, None, :].to_broadcast([P, 2, P]), ALU.mult).then_inc(s_ready, 1)
                dve.wait_ge(m_prod, b + 1)
                dve.tensor_tensor(shift[:, :], small[:, 8:8 + HALVES], gmean[:, :], ALU.add)
                dve.tensor_scalar(m_mat[:, :, :], prod[:, 2, :].rearrange("p (a c) -> p a c", a=HALVES),
                                  1.0 / Y_SCALE, None, ALU.mult).then_inc(m_ready, 1)

                with dve.Fori(0, BLOCKS) as k:
                    g = b * BLOCKS + k
                    src = y_block(g)
                    for u in range(UNITS):
                        n = UNITS * g + u
                        half, part = u % 2, u // 2
                        dve.wait_ge(evacuated, GRANT + n + 1)
                        if half == 0:
                            dve.wait_ge(mixed, n + 2)
                        v = src[:, :, half, part * UTOK:(part + 1) * UTOK]
                        dve.scalar_tensor_tensor(v, v, x_scale[:, half:half + 1],
                                                 scratch[:, u % 2, :][:, None, :], ALU.mult, ALU.add).then_inc(added, 1)
                    if more:
                        g2 = g + BLOCKS
                        dve.wait_ge(refill_in, 16 * (g + 1))
                        block_stats(g2, k, range(8))
                if more:
                    finish_stats(b + 1)
                    assert count[1] == IMAGE_OWN

            images(dve, image)

        @block.tensor
        def _(pe):
            pe.wait_ge(consts_in, 16 * 9)
            pe.wait_ge(setup_lk, 1)
            for t in range(PAIRS):
                for a in range(HALVES):
                    o = prod[:, a, 0:KV].rearrange("p (v x) -> p v x", v=2)[:, :, 30 * t:30 * t + 30]
                    pe.matmul(o, wt[:, t, a * P:(a + 1) * P], hel, start=True, stop=True)
                o = prod[0:3, 2, 0:KV].rearrange("p (v x) -> p v x", v=2)[:, :, 30 * t:30 * t + 30]
                ins = pe.matmul(o, b3[:, t, :], hel, start=True, stop=True)
            ins.then_inc(setup_w, 1)
            for t in range(PAIRS):
                r = 32 * (t % 4)
                ins = pe.matmul(acc[r:r + 32, t // 4, 0:C + 1], lk[:, t, :], wt[:, t, :], start=True, stop=True)
            ins.then_inc(setup_g, 1)
            pe.wait_ge(setup_done, 1)
            pe.wait_ge(evacuated, GRANT)

            def group_stats(b):
                pe.wait_ge(chan_ready, 2 * b + 1)
                pe.matmul(small[:, 0:HALVES], avg, chan[:, :, 0], start=True, stop=True).then_inc(group_sum, 1)
                pe.wait_ge(chan_ready, 2 * b + 2)
                pe.matmul(small[:, 0:HALVES], avg, dev[:, :], start=True, stop=True).then_inc(group_sum, 1)

            def accumulate(n, j, start, stop):
                pe.wait_ge(v_scaled, n + 1)
                for t in range(GT):
                    for g in range(2):
                        ins = pe.matmul(acc[:, g, 0:P],
                                        kv[:, j % 4, t, 8 * g:8 * g + 8, :],
                                        kv[:, j % 4, t, HEADS + 8 * g:HEADS + 8 * g + 8, :],
                                        start=start and t == 0, stop=stop and t == GT - 1,
                                        skip_group_check=True)
                ins.then_inc(kv_done, 1)

            def project(n, j):
                for t in range(GT):
                    o = prod[:, 2 * (j % 2) + t, 0:KV]
                    pe.matmul(o, ones_rows[:, :], bias_rows[:, :], start=True, stop=False)
                    tok = (j % SPQ) * GT * TILE + t * TILE
                    for a in range(HALVES):
                        hi = y_hi[:, j // SPQ, a, tok:tok + TILE]
                        lo = y_lo[:, j // SPQ, a, tok:tok + TILE]
                        pe.matmul(o, hi, w_hi[:, a, :], start=False, stop=False)
                        pe.matmul(o, hi, w_lo[:, a, :], start=False, stop=False)
                        ins = pe.matmul(o, lo, w_hi[:, a, :], start=False, stop=a == HALVES - 1)
                ins.then_inc(projected, 1)

            def image(b, more):
                pe.wait_ge(evacuated, GRANT + UNITS * BLOCKS * b)

                def body(k, first, last):
                    g = b * BLOCKS + k
                    n0 = g * STEPS
                    for j in range(STEPS):
                        if j % SPQ == 0:
                            pe.wait_ge(split_ready, QUARTERS * g + j // SPQ + 1)
                        if not (first and j < 2):
                            pe.wait_ge(copied, n0 + j - 1)
                        project(n0 + j, j)
                        if not (first and j < 2):
                            accumulate(n0 + j - 2, (j - 2) % STEPS, first and j == 2, False)
                    if last:
                        accumulate(n0 + STEPS - 2, STEPS - 2, False, False)
                        accumulate(n0 + STEPS - 1, STEPS - 1, False, True)
                blocks(pe, body)

                pe.wait_ge(s_ready, b + 1)
                pe.wait_ge(copied, ISTEPS * (b + 1))
                for g in range(2):
                    ins = pe.matmul(prod[:, g, 0:C + 1], s_mat[:, g, :], g_mat[:, g, :], start=True, stop=True)
                ins.then_inc(u_prod, 1)
                pe.wait_ge(u_ready, b + 1)
                for g in range(2):
                    for a in range(HALVES):
                        pe.matmul(prod[:, 2, a * C + g * P:a * C + (g + 1) * P],
                                  u_mat[:, g, a * P:(a + 1) * P], l_mat[:, g, :], start=True, stop=True)
                for g in range(2):
                    ins = pe.matmul(small[:, 8 + g:9 + g], l_mat[:, g, :], u_mat[:, g, C:C + 1], start=True, stop=True)
                ins.then_inc(m_prod, 1)

                with pe.Fori(0, BLOCKS) as k:
                    g = b * BLOCKS + k
                    src = y_block(g)
                    pe.wait_ge(m_ready, b + 1)
                    for u in range(UNITS):
                        n = UNITS * g + u
                        half, part = u % 2, u // 2
                        pe.wait_ge(evacuated, n + 1)
                        for p in range(2):
                            tok = part * UTOK + p * 512
                            for a in range(HALVES):
                                ins = pe.matmul(prod[:, 2 * (u % 2) + p, :],
                                                m_mat[:, a, half * P:(half + 1) * P],
                                                src[:, :, a, tok:tok + 512].rearrange("p s n -> p (s n)"),
                                                start=a == 0, stop=a == HALVES - 1)
                        ins.then_inc(mixed, 1)
                if more:
                    group_stats(b + 1)

            group_stats(0)
            images(pe, image)


def _tables():
    import numpy as np
    q = np.zeros((D, J))
    for j in range(J):
        q[:j + 1, j] = 1.0 / np.sqrt((j + 1) * (j + 2))
        q[j + 1, j] = -(j + 1) / np.sqrt((j + 1) * (j + 2))
    t = np.zeros((P, C_WIDTH))
    for h in range(2):
        for kind in range(2):
            r = 48 * h + 16 * (1 + kind)
            t[r:r + D, C_HEL + 30 * kind + J * h:C_HEL + 30 * kind + J * (h + 1)] = q
        t[48 * h:48 * h + D, C_QG + 16 * h:C_QG + 16 * h + J] = q
        t[48 * h:48 * h + D, C_EG + 16 * h + J] = 1.0
    for h in range(8):
        s = slice(16 * h, 16 * h + 16)
        t[16 * h:16 * h + J, C_QL + 16 * h:C_QL + 16 * h + 16] = q.T
        t[16 * h + J, C_EL + 16 * h:C_EL + 16 * h + 16] = 1.0
        t[s, C_MASK + 16 * h:C_MASK + 16 * h + 16] = 1.0 / N
    for g in range(P // GROUP):
        t[GROUP * g:GROUP * (g + 1), C_AVG + GROUP * g:C_AVG + GROUP * (g + 1)] = 1.0 / GROUP
    for i in range(3):
        t[i + 1:3, C_E3 + i] = 1.0
    return t.astype(np.float32)


_INS = ["x", "L0_conv_w_qkv", "L0_conv_b_qkv", "L0_conv_kln_w", "L0_conv_kln_b", "L0_conv_vln_w", "L0_conv_vln_b"]


def kernel(**inputs):
    import numpy as _np
    import concourse.bacc as _bacc
    from concourse import mybir as _mybir
    from concourse.bass_utils import run_bass_kernel_spmd as _run

    nc = _bacc.Bacc("TRN2", target_bir_lowering=False, num_devices=1)
    arrays, args = {}, []
    for name in _INS:
        a = _np.ascontiguousarray(inputs[name])
        arrays[f"in_{name}"] = a
        args.append(nc.dram_tensor(f"in_{name}", a.shape, _mybir.dt.from_np(a.dtype), kind="ExternalInput").ap())
    tables = _tables()
    arrays["in_tables"] = tables
    args.append(nc.dram_tensor("in_tables", tables.shape, fp32, kind="ExternalInput").ap())
    args.append(nc.dram_tensor("out_0", (B, C, H, W), fp32, kind="ExternalOutput").ap())
    build(nc, *args)
    r = _run(nc, [arrays], core_ids=[0])
    return r.results[0]["out_0"]
```

```python
from contextlib import ExitStack

import concourse.bass as bass
from concourse import mybir

B, C, H, W = 8, 256, 128, 128
N = H * W
HEADS, D = 16, 16
J = D - 1
P = 128
HALVES = C // P
NG = 32
GROUP = C // NG
PAIR = 2 * 3 * D
PAIRS = HEADS // 2
GN_EPS, LN_EPS = 1e-5, 1e-5

SLOT = 1024
ISLOTS = N // SLOT
SLOTS = ISLOTS + 3
BLOCK = 2048
PARTS = BLOCK // SLOT
BLOCKS = N // BLOCK
QTOK = 512
QUARTERS = BLOCK // QTOK
QPP = QUARTERS // PARTS
IQ = QUARTERS * BLOCKS
TILE = 128
GT = 2
STEPS = BLOCK // (TILE * GT)
SPQ = STEPS // QUARTERS
ISTEPS = STEPS * BLOCKS
KV = 2 * HEADS * J
UNITS = 2 * PARTS
IU = UNITS * BLOCKS
IMAGE_OWN = 8
GRANT = 2
Y_SCALE = 64.0
W_SCALE = 1024.0
M_SCALE = 1024.0
TINY = 1e-30

C_MASK, C_AVG, C_KEPT = 0, 128, 256
C_HEL, C_QG, C_EG, C_QL, C_EL, C_E3 = 256, 316, 348, 380, 508, 636
C_WIDTH = 640

fp32 = mybir.dt.float32
fp16 = mybir.dt.float16
bf16 = mybir.dt.bfloat16
ALU = mybir.AluOpType
ACT = mybir.ActivationFunctionType
AX = mybir.AxisListType
RMAX = bass.bass_isa.ReduceOp.max


def build(nc, x, w_qkv, b_qkv, kln_w, kln_b, vln_w, vln_b, consts, out):
    x_v = x.rearrange("b (a p) h w -> b p a (h w)", p=P)
    out_v = out.rearrange("b (a p) h w -> b p a (h w)", p=P)

    ctx = ExitStack()
    with ctx:
        def sb(name, shape, dt):
            return ctx.enter_context(nc.sbuf_tensor(name, shape, dt))

        def sem(name):
            return ctx.enter_context(nc.semaphore(name))

        ring = sb("ring", [P, SLOTS, HALVES, SLOT], fp32)
        y_hi = sb("y_hi", [P, QUARTERS, HALVES, QTOK], fp16)
        y_lo = sb("y_lo", [P, QUARTERS, HALVES, QTOK], fp16)
        kv = sb("kv", [P, 4, GT, 2 * HEADS, D], fp32)
        scratch = sb("scratch", [P, 2, SLOT], fp32)
        sigma = sb("sigma", [P, 4, GT, 2 * HEADS], fp32)
        sig_kv = sb("sig_kv", [P, 4, GT, HEADS], fp32)
        inv_kv = sb("inv_kv", [P, 4, GT, HEADS], fp32)
        w_hi = sb("w_hi", [P, HALVES, KV], fp16)
        w_lo = sb("w_lo", [P, HALVES, KV], fp16)
        bias_rows = sb("bias_rows", [P, KV], bf16)
        ones_rows = sb("ones_rows", [P, P], bf16)
        eps_h = sb("eps_h", [P, 2 * HEADS], fp32)
        tab = sb("tab", [P, C_KEPT], fp32)
        g_mat = sb("g_mat", [P, 2, C + 1], fp32)
        l_mat = sb("l_mat", [P, 2, P], fp32)
        kv_flat = kv[:, :, :, :, :].rearrange("p i t h j -> p (i t h j)")
        s_mat = kv_flat[:, 0:2 * P].rearrange("p (g n) -> p g n", g=2)
        u_mat = kv_flat[:, 1024:1024 + 2 * (C + 1)].rearrange("p (g n) -> p g n", g=2)
        m_hi = sb("m_hi", [P, HALVES, C], fp16)
        m_lo = sb("m_lo", [P, HALVES, C], fp16)
        gl_max = sb("gl_max", [P, 4], fp32)
        gl_scale = sb("gl_scale", [P, 4], fp32)
        gl_inv = sb("gl_inv", [P, 4], fp32)
        row_scale = sb("row_scale", [P, 2], fp32)
        out_scale = sb("out_scale", [P, 2], fp32)
        shift = sb("shift", [P, HALVES], fp32)
        stats = sb("stats", [P, HALVES, N // 512, 6], fp32)
        chan = sb("chan", [P, HALVES, 2], fp32)
        dev = sb("dev", [P, HALVES], fp32)
        dev2 = sb("dev2", [P, HALVES], fp32)
        gmean = sb("gmean", [P, HALVES], fp32)
        gvar = sb("gvar", [P, HALVES], fp32)
        std = sb("std", [P, HALVES], fp32)
        rstd = sb("rstd", [P, HALVES], fp32)
        y_scale = sb("y_scale", [P, HALVES], fp32)
        x_scale = sb("x_scale", [P, HALVES], fp32)

        room = ring[:, SLOTS - 2:SLOTS, :, :].rearrange("p s a n -> p (s a n)")
        at = [0]

        def setup_room(rows, width):
            at[0] += width
            assert at[0] <= 2 * HALVES * SLOT
            return room[0:rows, at[0] - width:at[0]]

        tab2 = setup_room(P, C_WIDTH - C_KEPT)
        wt = setup_room(PAIR, PAIRS * (C + 1)).rearrange("p (t n) -> p t n", t=PAIRS)
        b3 = setup_room(PAIR, PAIRS * 3).rearrange("p (t n) -> p t n", t=PAIRS)
        klw = setup_room(PAIR, PAIRS)
        klb = setup_room(PAIR, PAIRS)
        lk = setup_room(PAIR, PAIRS * 32).rearrange("p (t n) -> p t n", t=PAIRS)
        vlw = setup_room(P, C)
        vlb = setup_room(P, C)
        wmax = setup_room(P, HALVES * 32).rearrange("p (a n) -> p a n", a=HALVES)
        bmax = setup_room(3, 32)
        amax = setup_room(P, 32)
        alpha = setup_room(P, 32)
        w0 = C_WIDTH - C_KEPT
        ws = room[:, w0:w0 + KV]
        bs = room[0:3, w0 + KV:w0 + 2 * KV]
        bpart = room[0:3, w0 + 2 * KV:w0 + 3 * KV]

        prod = ctx.enter_context(nc.psum_tensor("prod", [P, 4, 512], fp32))
        acc = ctx.enter_context(nc.psum_tensor("acc", [P, 2, 512], fp32))
        small = ctx.enter_context(nc.psum_tensor("small", [P, 512], fp32))

        hel = tab2[0:PAIR, C_HEL - C_KEPT:C_HEL - C_KEPT + 60].rearrange("p (v x) -> p v x", v=2)
        avg = tab[:, C_AVG:C_AVG + P]
        mask = tab[:, C_MASK:C_MASK + P]

        consts_in = sem("consts_in")
        setup_cleared = sem("setup_cleared")
        setup_w = sem("setup_w")
        setup_g = sem("setup_g")
        setup_lk = sem("setup_lk")
        setup_amax = sem("setup_amax")
        setup_wmax = sem("setup_wmax")
        setup_b3 = sem("setup_b3")
        setup_rows = sem("setup_rows")
        setup_scale = sem("setup_scale")
        setup_done = sem("setup_done")
        first_in = [sem(f"first_in{i}") for i in range(ISLOTS)]
        refill_in = [sem("refill_in_even"), sem("refill_in_odd")]
        stored = [sem("stored_even"), sem("stored_odd")]
        chan_ready = sem("chan_ready")
        group_sum = sem("group_sum")
        var_ready = sem("var_ready")
        std_ready = sem("std_ready")
        normed = sem("normed")
        hi_ready = sem("hi_ready")
        split_ready = sem("split_ready")
        projected = sem("projected")
        squared = sem("squared")
        copied = sem("copied")
        summed = sem("summed")
        sigma_ready = sem("sigma_ready")
        sig_kv_ready = sem("sig_kv_ready")
        v_scaled = sem("v_scaled")
        kv_done = sem("kv_done")
        s_ready = sem("s_ready")
        u_prod = sem("u_prod")
        u_ready = sem("u_ready")
        m_prod = sem("m_prod")
        m_ready = sem("m_ready")
        shift_ready = sem("shift_ready")
        mixed = sem("mixed")
        shifted = sem("shifted")
        added = sem("added")
        pool_sig = sem("pool_sig")
        act_setup = sem("act_setup")
        inv_ready = sem("inv_ready")
        stats_done = sem("stats_done")
        carried = {e.engine: sem(f"carried_{n}") for n, e in (("sp", nc.sync), ("act", nc.scalar), ("pool", nc.gpsimd))}
        dve_step = sem("dve_step")

        block = ctx.enter_context(nc.Block())

        def slot(i):
            return ring[:, i % SLOTS:i % SLOTS + 1, :, :] if isinstance(i, int) else \
                ring[:, bass.ds(i % SLOTS, 1), :, :]

        def quarter(b, k, q):
            tok = (q % QPP) * QTOK
            return slot((b * BLOCKS + k) * PARTS + q // QPP)[:, :, :, tok:tok + QTOK]

        def settled(eng):
            eng.sem_inc(carried[eng.engine], 1)

        def images(eng, body):
            with eng.Fori(0, B - 1) as b:
                body(b, True)
            body(B - 1, False)

        def blocks(eng, body):
            body(0, True, False)
            with eng.Fori(1, BLOCKS - 1) as k:
                body(k, False, False)
            body(BLOCKS - 1, False, True)

        @block.sync
        def _(sp):
            sp.dma_start(tab[:, :], consts[:, 0:C_KEPT]).then_inc(consts_in, 16)
            sp.dma_start(tab2, consts[:, C_KEPT:]).then_inc(consts_in, 16)
            with nc.allow_non_contiguous_dma(reason="small parameters"):
                sp.dma_start(wt[:, :, 0:C], w_qkv.rearrange("(t p) c -> p t c", p=PAIR)).then_inc(consts_in, 16)
                sp.dma_start(wt[:, :, C:C + 1], b_qkv.rearrange("(t p one) -> p t one", p=PAIR, one=1)).then_inc(consts_in, 16)
                sp.dma_start(vlw, vln_w.rearrange("(one h) d -> one (h d)", one=1).to_broadcast([P, C])).then_inc(consts_in, 16)
                sp.dma_start(vlb, vln_b.rearrange("(one h) d -> one (h d)", one=1).to_broadcast([P, C])).then_inc(consts_in, 16)
                sp.wait_ge(setup_cleared, 1)
                for row in range(2):
                    q0 = row * 3 * D
                    sp.dma_start(klw[q0:q0 + D, :], kln_w.rearrange("(t r) d -> r d t", r=2)[row]).then_inc(consts_in, 16)
                    sp.dma_start(klb[q0:q0 + D, :], kln_b.rearrange("(t r) d -> r d t", r=2)[row]).then_inc(consts_in, 16)
            for i in range(ISLOTS):
                if i >= 4:
                    sp.wait_ge(first_in[i - 4], 16)
                sp.dma_start(ring[:, i, :, :], x_v[0, :, :, i * SLOT:(i + 1) * SLOT]).then_inc(first_in[i], 16)
            sp.dma_start(ring[:, ISLOTS, :, :], x_v[1, :, :, 0:SLOT]).then_inc(refill_in[0], 16)
            sp.wait_ge(setup_done, 1)
            sp.dma_start(ring[:, ISLOTS + 1, :, :], x_v[1, :, :, SLOT:2 * SLOT]).then_inc(refill_in[1], 16)

            ring_flat = ring[:, :, :, :].rearrange("p s a n -> p (s a n)")

            def slot_at(i):
                return ring_flat[:, bass.ds((i % SLOTS) * (HALVES * SLOT), HALVES * SLOT)]\
                    .rearrange("p (a n) -> p a n", a=HALVES)

            def tokens_at(t, pair, odd):
                o = (pair // (ISLOTS // 2)) * (C * N) + (pair % (ISLOTS // 2)) * (2 * SLOT) + odd * SLOT
                return bass.AP(tensor=t.tensor, offset=o, ap=[[N, P], [P * N, HALVES], [1, SLOT]])

            def store(i, odd):
                sp.wait_ge(added, GRANT + 4 * i + 2 * odd + 2)
                settled(sp)
                sp.dma_start(tokens_at(out, i, odd), slot_at(2 * i + odd)).then_inc(stored[odd], 16)

            def refill(i, odd):
                sp.wait_ge(stored[1 - odd], 16 * (i - ISLOTS // 2))
                sp.wait_ge(refill_in[odd], 16 * (i - ISLOTS // 2))
                settled(sp)
                sp.dma_start(slot_at(2 * i + odd), tokens_at(x, i, odd)).then_inc(refill_in[odd], 16)

            with sp.Fori(0, (B - 1) * ISLOTS // 2 - 1) as i:
                store(i, 0)
                refill(i + ISLOTS // 2 + 1, 0)
                store(i, 1)
                refill(i + ISLOTS // 2 + 1, 1)
            with sp.Fori((B - 1) * ISLOTS // 2 - 1, B * ISLOTS // 2) as i:
                store(i, 0)
                sp.wait_ge(stored[1], 16 * (i + 1))
                settled(sp)
                store(i, 1)
                sp.wait_ge(stored[0], 16 * (i + 1))
                settled(sp)
            sp.wait_ge(stored[0], 16 * (B * ISLOTS // 2))
            sp.wait_ge(stored[1], 16 * (B * ISLOTS // 2 + 1))

        @block.gpsimd
        def _(pool):
            nc.gpsimd.memset(klw, 0.0)
            nc.gpsimd.memset(klb, 0.0).then_inc(setup_cleared, 1)
            pool.wait_ge(setup_wmax, 1)
            nc.gpsimd.partition_all_reduce(amax, wmax[:, 0, :], P, RMAX).then_inc(setup_amax, 1)

            def lows(phase, b, k, q):
                pool.wait_ge(hi_ready, IQ * (2 * b + phase) + QUARTERS * k + q + 1)
                settled(pool)
                nc.gpsimd.tensor_tensor(y_lo[:, q:q + 1, :, :], quarter(b, k, q),
                                        y_hi[:, q:q + 1, :, :], ALU.subtract).then_inc(split_ready, 1)

            def sigmas(n, j):
                pool.wait_ge(sigma_ready, n + 1)
                s16 = kv[:, j % 4, :, :, J]
                nc.gpsimd.tensor_tensor(s16, sigma[:, j % 4, :, :],
                                        eps_h[:, None, :].to_broadcast([P, GT, 2 * HEADS]),
                                        ALU.add).then_inc(pool_sig, 1)
                pool.wait_ge(pool_sig, n + 1)
                nc.gpsimd.tensor_tensor(sig_kv[:, j % 4, :, :], kv[:, j % 4, :, 0:HEADS, J],
                                        kv[:, j % 4, :, HEADS:, J], ALU.mult).then_inc(sig_kv_ready, 1)

            def image(b, more):
                for q in range(2):
                    lows(0, b, 0, q)

                def body(k, first, last):
                    n0 = (b * BLOCKS + k) * STEPS
                    for j in range(STEPS):
                        sigmas(n0 + j, j)
                        if j % SPQ == SPQ - 1:
                            q = j // SPQ + 2
                            if q < QUARTERS:
                                lows(0, b, k, q)
                            elif not last:
                                lows(0, b, k + 1, q - QUARTERS)
                blocks(pool, body)

                for q in range(QPP):
                    lows(1, b, 0, q)
                with pool.Fori(0, BLOCKS - 1) as k:
                    for q in range(QUARTERS):
                        if q + QPP < QUARTERS:
                            lows(1, b, k, q + QPP)
                        else:
                            lows(1, b, k + 1, q + QPP - QUARTERS)
                for q in range(QPP, QUARTERS):
                    lows(1, b, BLOCKS - 1, q)

            images(pool, image)

        @block.scalar
        def _(act):
            act.wait_ge(setup_g, 1)
            nc.scalar.activation(g_mat[:, 0, :], acc[:, 0, 0:C + 1], ACT.Copy).then_inc(act_setup, 1)
            nc.scalar.activation(g_mat[:, 1, :], acc[:, 1, 0:C + 1], ACT.Copy).then_inc(act_setup, 1)

            def group_std(b):
                act.wait_ge(var_ready, b + 1)
                nc.scalar.activation(std[:, :], gvar[:, :], ACT.Sqrt).then_inc(std_ready, 1)

            def highs(b, k, q, waits):
                act.wait_ge(normed, IQ * b + QUARTERS * k + q + 1)
                if waits:
                    act.wait_ge(projected, SPQ * (IQ * b + QUARTERS * k + q - QUARTERS + 1))
                settled(act)
                nc.scalar.activation(y_hi[:, q:q + 1, :, :], quarter(b, k, q), ACT.Copy).then_inc(hi_ready, 1)

            def highs_again(b, k, q, first):
                if first:
                    act.wait_ge(projected, SPQ * (IQ * b + IQ - QUARTERS + q + 1))
                else:
                    act.wait_ge(mixed, IU * b + UNITS * k - UNITS + 2 * (q // QPP) + 2)
                settled(act)
                nc.scalar.activation(y_hi[:, q:q + 1, :, :], quarter(b, k, q), ACT.Copy).then_inc(hi_ready, 1)

            def image(b, more):
                for q in range(2):
                    highs(b, 0, q, False)

                def body(k, first, last):
                    n0 = (b * BLOCKS + k) * STEPS
                    for j in range(STEPS):
                        n = n0 + j
                        z = prod[:, 2 * (j % 2):2 * (j % 2) + 2, 0:KV]
                        act.wait_ge(projected, n + 1)
                        if not (first and j < 2):
                            act.wait_ge(summed, n - 1)
                        nc.scalar.activation(
                            scratch[:, j % 2, 0:GT * KV].rearrange("p (t n) -> p t n", t=GT), z,
                            ACT.Square).then_inc(squared, 1)
                        if not (first and j < 4):
                            act.wait_ge(kv_done, n - 3)
                        nc.scalar.activation(
                            kv[:, j % 4, :, :, 0:J],
                            z.rearrange("p t (h j) -> p t h j", j=J), ACT.Copy).then_inc(copied, 1)
                        act.wait_ge(summed, n + 1)
                        nc.scalar.activation(sigma[:, j % 4, :, :], sigma[:, j % 4, :, :], ACT.Sqrt,
                                             scale=1.0 / (D - 1)).then_inc(sigma_ready, 1)
                        if j % SPQ == SPQ - 1:
                            q = j // SPQ + 2
                            if q < QUARTERS:
                                highs(b, k, q, not first)
                            elif not last:
                                highs(b, k + 1, q - QUARTERS, True)
                blocks(act, body)

                for q in range(QPP):
                    highs_again(b, 0, q, True)

                act.wait_ge(u_prod, b + 1)
                nc.scalar.activation(u_mat, prod[:, 0:2, 0:C + 1], ACT.Copy).then_inc(u_ready, 1)

                def body_b(k, first, last):
                    for u in range(UNITS):
                        n = IU * b + UNITS * k + u
                        part, half = u // 2, u % 2
                        if first and u == 0:
                            act.wait_ge(shift_ready, b + 1)
                        act.wait_ge(added, n + 1)
                        settled(act)
                        nc.scalar.activation(
                            scratch[:, half:half + 1, :], slot((b * BLOCKS + k) * PARTS + part)[:, :, half, :],
                            ACT.Identity, scale=x_scale[:, half:half + 1],
                            bias=shift[:, half:half + 1]).then_inc(shifted, 1)
                        q = QPP * part + QPP + half
                        if q < QUARTERS:
                            highs_again(b, k, q, first)
                        elif not last:
                            highs_again(b, k + 1, q - QUARTERS, False)
                blocks(act, body_b)
                if more:
                    group_std(b + 1)

            group_std(0)
            images(act, image)

        @block.vector
        def _(dve):
            count = [0, 0]

            def own(ins):
                count[1] += 1
                ins.then_inc(dve_step, 1)
                dve.wait_ge(dve_step, count[0] + count[1])

            dve.memset(bias_rows[:, :], 0.0)
            dve.memset(ones_rows[:, :], 1.0)
            dve.wait_ge(consts_in, 16 * 10)
            own(dve.tensor_copy(b3, wt[:, :, C:C + 1].to_broadcast([PAIR, PAIRS, 3])))
            qg = tab2[0:PAIR, C_QG - C_KEPT:C_QG - C_KEPT + 32]
            eg = tab2[0:PAIR, C_EG - C_KEPT:C_EG - C_KEPT + 32]
            for t in range(PAIRS):
                own(dve.tensor_scalar(lk[:, t, :], qg, klw[:, t:t + 1], None, ALU.mult))
            for t in range(PAIRS):
                ins = dve.scalar_tensor_tensor(lk[:, t, :], eg, klb[:, t:t + 1], lk[:, t, :], ALU.mult, ALU.add)
            ins.then_inc(setup_lk, 1)
            for g in range(2):
                own(dve.tensor_tensor(l_mat[:, g, :], tab2[:, C_QL - C_KEPT:C_QL - C_KEPT + P], vlw[:, g * P:(g + 1) * P], ALU.mult))
                own(dve.tensor_tensor(vlb[:, g * P:(g + 1) * P], tab2[:, C_EL - C_KEPT:C_EL - C_KEPT + P], vlb[:, g * P:(g + 1) * P], ALU.mult))
                own(dve.tensor_tensor(l_mat[:, g, :], l_mat[:, g, :], vlb[:, g * P:(g + 1) * P], ALU.add))
            dve.wait_ge(setup_w, 1)
            for a in range(HALVES):
                own(dve.tensor_reduce(wmax[:, a, :], prod[:, a, 0:KV].rearrange("p (h j) -> p h j", j=J),
                                      AX.X, ALU.max, apply_absolute_value=True))
            own(dve.tensor_reduce(bmax, prod[0:3, 2, 0:KV].rearrange("p (h j) -> p h j", j=J),
                                  AX.X, ALU.max, apply_absolute_value=True))
            own(dve.tensor_tensor(wmax[:, 0, :], wmax[:, 0, :], wmax[:, 1, :], ALU.max))
            dve.tensor_tensor(wmax[0:3, 0, :], wmax[0:3, 0, :], bmax, ALU.max).then_inc(setup_wmax, 1)
            dve.wait_ge(setup_amax, 1)
            own(dve.tensor_scalar(amax, amax, TINY, None, ALU.max))
            own(dve.reciprocal(alpha, amax))
            own(dve.tensor_scalar(eps_h[:, :], alpha, LN_EPS * W_SCALE * Y_SCALE, None, ALU.mult))
            own(dve.tensor_scalar(alpha, alpha, W_SCALE, None, ALU.mult))
            dve.wait_ge(act_setup, 2)
            own(dve.tensor_reduce(gl_max[:, 0:2], g_mat[:, :, 0:C], AX.X, ALU.max, apply_absolute_value=True))
            dve.tensor_reduce(gl_max[:, 2:4], l_mat[:, :, :], AX.X, ALU.max, apply_absolute_value=True).then_inc(setup_rows, 1)
            dve.wait_ge(setup_scale, 1)
            own(dve.tensor_scalar(gl_scale[:, :], small[:, 0:4], float(N), TINY, ALU.mult, ALU.max))
            own(dve.reciprocal(gl_inv[:, :], gl_scale[:, :]))
            for g in range(2):
                own(dve.tensor_scalar(g_mat[:, g, :], g_mat[:, g, :], gl_inv[:, g:g + 1], None, ALU.mult))
                own(dve.tensor_scalar(l_mat[:, g, :], l_mat[:, g, :], gl_inv[:, 2 + g:3 + g], None, ALU.mult))
            own(dve.tensor_tensor(row_scale[:, :], gl_scale[:, 0:2], gl_scale[:, 2:4], ALU.mult))
            own(dve.tensor_scalar(out_scale[:, :], row_scale[:, :], 1.0 / (M_SCALE * Y_SCALE), None, ALU.mult))
            for a in range(HALVES):
                own(dve.tensor_tensor(ws.rearrange("p (h j) -> p h j", j=J),
                                      prod[:, a, 0:KV].rearrange("p (h j) -> p h j", j=J),
                                      alpha[:, :, None].to_broadcast([P, 2 * HEADS, J]), ALU.mult))
                own(dve.tensor_copy(w_hi[:, a, :], ws))
                own(dve.tensor_tensor(w_lo[:, a, :], ws, w_hi[:, a, :], ALU.subtract))
            own(dve.tensor_tensor(bs.rearrange("p (h j) -> p h j", j=J),
                                  prod[0:3, 2, 0:KV].rearrange("p (h j) -> p h j", j=J),
                                  alpha[0:3, :, None].to_broadcast([3, 2 * HEADS, J]), ALU.mult))
            own(dve.tensor_scalar(bs, bs, Y_SCALE, None, ALU.mult))
            below = tab2[0:3, C_E3 - C_KEPT:C_E3 - C_KEPT + 3]
            for i in range(3):
                own(dve.tensor_copy(bias_rows[0:3, :], bs))
                if i < 2:
                    own(dve.tensor_scalar(bpart, bias_rows[0:3, :], below[:, i:i + 1], None, ALU.mult))
                    own(dve.tensor_tensor(bs, bs, bpart, ALU.subtract))
            dve.tensor_copy(gmean[:, :], tab[:, 0:HALVES]).then_inc(added, GRANT)
            dve.tensor_copy(dev[:, :], tab[:, 0:HALVES]).then_inc(stored[1], 16)
            dve.tensor_copy(gvar[:, :], tab[:, 0:HALVES]).then_inc(setup_done, 1)

            def slot_stats(i, k, part, pieces):
                for p in pieces:
                    a, h = p % 2, p // 2
                    at = part * (SLOT // 512) + h
                    o = stats[:, a, k * (BLOCK // 512) + at, :] if isinstance(k, int) else \
                        stats[:, a, bass.ds(k * (BLOCK // 512) + at, 1), :]
                    v = slot(i)[:, 0, a, h * 512:(h + 1) * 512] if isinstance(i, int) else \
                        slot(i)[:, :, a, h * 512:(h + 1) * 512]
                    dve.bn_stats(o, v).then_inc(stats_done, 1)

            def finish_stats(b):
                dve.wait_ge(stats_done, 64 * (b + 1))
                dve.memset(dev[:, :], 0.0)
                for a in range(HALVES):
                    ins = dve.bn_aggr(chan[:, a, :], stats[:, a, :, :])
                ins.then_inc(chan_ready, 1)
                dve.wait_ge(group_sum, 2 * b + 1)
                own(dve.tensor_copy(gmean[:, :], small[:, 0:HALVES]))
                own(dve.tensor_tensor(dev[:, :], chan[:, :, 0], gmean[:, :], ALU.subtract))
                own(dve.tensor_tensor(dev2[:, :], dev[:, :], dev[:, :], ALU.mult))
                dve.tensor_tensor(dev[:, :], dev2[:, :], chan[:, :, 1], ALU.add).then_inc(chan_ready, 1)
                dve.wait_ge(group_sum, 2 * b + 2)
                dve.tensor_scalar(gvar[:, :], small[:, 0:HALVES], GN_EPS, None, ALU.add).then_inc(var_ready, 1)
                dve.wait_ge(std_ready, b + 1)
                own(dve.reciprocal(rstd[:, :], std[:, :]))
                own(dve.tensor_scalar(y_scale[:, :], rstd[:, :], Y_SCALE, None, ALU.mult))
                own(dve.tensor_scalar(x_scale[:, :], std[:, :], 1.0 / Y_SCALE, None, ALU.mult))

            def normalise(b, k, q):
                for a in range(HALVES):
                    v = quarter(b, k, q)[:, :, a, :]
                    ins = dve.tensor_scalar(v, v, gmean[:, a:a + 1], y_scale[:, a:a + 1],
                                            ALU.subtract, ALU.mult)
                ins.then_inc(normed, 1)

            def sum_squares(n, j):
                dve.wait_ge(squared, n + 1)
                dve.tensor_reduce(sigma[:, j % 4, :, :],
                                  scratch[:, j % 2, 0:GT * KV].rearrange("p (t h j) -> p t h j", t=GT, j=J),
                                  AX.X, ALU.add).then_inc(summed, 1)

            def scale_v(n, j):
                dve.wait_ge(sig_kv_ready, n + 1)
                dve.reciprocal(kv[:, j % 4, :, HEADS:, J], kv[:, j % 4, :, 0:HEADS, J])
                dve.reciprocal(inv_kv[:, j % 4, :, :], sig_kv[:, j % 4, :, :]).then_inc(inv_ready, 1)
                dve.wait_ge(copied, n + 1)
                dve.wait_ge(inv_ready, n + 1)
                for t in range(GT):
                    v = kv[:, j % 4, t, HEADS:, 0:J]
                    ins = dve.tensor_tensor(v, v, inv_kv[:, j % 4, t, :, None].to_broadcast([P, HEADS, J]), ALU.mult)
                ins.then_inc(v_scaled, 1)

            for i in range(ISLOTS):
                dve.wait_ge(first_in[i], 16)
                slot_stats(i, i // PARTS, i % PARTS, range(4))
            finish_stats(0)
            setup_steps = count[1]

            def image(b, more):
                count[0], count[1] = b * IMAGE_OWN + setup_steps, 0
                for q in range(3):
                    normalise(b, 0, q)

                def body(k, first, last):
                    n0 = (b * BLOCKS + k) * STEPS
                    for j in range(STEPS):
                        sum_squares(n0 + j, j)
                        if j == 0:
                            normalise(b, k, 3)
                        elif j % SPQ == 0 and not last:
                            normalise(b, k + 1, j // SPQ - 1)
                        scale_v(n0 + j, j)
                blocks(dve, body)

                dve.wait_ge(kv_done, ISTEPS * (b + 1))
                dve.tensor_tensor(s_mat, acc[:, :, 0:P],
                                  mask[:, None, :].to_broadcast([P, 2, P]), ALU.mult).then_inc(s_ready, 1)
                dve.wait_ge(m_prod, b + 1)
                m_psum = prod[:, 2, :].rearrange("p (a c) -> p a c", a=HALVES)
                own(dve.tensor_scalar(m_hi[:, :, :], m_psum, M_SCALE, None, ALU.mult))
                dve.scalar_tensor_tensor(m_lo[:, :, :], m_psum, M_SCALE, m_hi[:, :, :], ALU.mult, ALU.subtract)\
                   .then_inc(m_ready, 1)
                own(dve.tensor_tensor(shift[:, :], small[:, 8:8 + HALVES], row_scale[:, :], ALU.mult))
                dve.tensor_tensor(shift[:, :], shift[:, :], gmean[:, :], ALU.add).then_inc(shift_ready, 1)

                with dve.Fori(0, BLOCKS) as k:
                    for u in range(UNITS):
                        n = IU * b + UNITS * k + u
                        part, half = u // 2, u % 2
                        i = (b * BLOCKS + k) * PARTS + part
                        dve.wait_ge(shifted, n + 1)
                        dve.wait_ge(mixed, n + 1)
                        dve.scalar_tensor_tensor(
                            slot(i)[:, :, half, :].rearrange("p s (t n) -> p (s t) n", t=2),
                            prod[:, 2 * half:2 * half + 2, :], out_scale[:, half:half + 1],
                            scratch[:, half, :].rearrange("p (t n) -> p t n", t=2),
                            ALU.mult, ALU.add).then_inc(added, 1)
                        if more:
                            if half == 0:
                                dve.wait_ge(refill_in[part], 16 * (b * BLOCKS + k + 1))
                            slot_stats(i + ISLOTS, k, part, range(2 * half, 2 * half + 2))
                if more:
                    finish_stats(b + 1)
                    assert count[1] == IMAGE_OWN

            images(dve, image)

        @block.tensor
        def _(pe):
            pe.wait_ge(consts_in, 16 * 10)
            pe.wait_ge(setup_lk, 1)
            for t in range(PAIRS):
                for a in range(HALVES):
                    o = prod[:, a, 0:KV].rearrange("p (v x) -> p v x", v=2)[:, :, 30 * t:30 * t + 30]
                    pe.matmul(o, wt[:, t, a * P:(a + 1) * P], hel, start=True, stop=True)
                o = prod[0:3, 2, 0:KV].rearrange("p (v x) -> p v x", v=2)[:, :, 30 * t:30 * t + 30]
                ins = pe.matmul(o, b3[:, t, :], hel, start=True, stop=True)
            ins.then_inc(setup_w, 1)
            for t in range(PAIRS):
                r = 32 * (t % 4)
                ins = pe.matmul(acc[r:r + 32, t // 4, 0:C + 1], lk[:, t, :], wt[:, t, :], start=True, stop=True)
            ins.then_inc(setup_g, 1)
            pe.wait_ge(setup_rows, 1)
            pe.matmul(small[:, 0:4], mask, gl_max[:, :], start=True, stop=True).then_inc(setup_scale, 1)
            pe.wait_ge(setup_done, 1)

            def group_stats(b):
                pe.wait_ge(chan_ready, 2 * b + 1)
                pe.matmul(small[:, 0:HALVES], avg, chan[:, :, 0], start=True, stop=True).then_inc(group_sum, 1)
                pe.wait_ge(chan_ready, 2 * b + 2)
                pe.matmul(small[:, 0:HALVES], avg, dev[:, :], start=True, stop=True).then_inc(group_sum, 1)

            def accumulate(n, j, start, stop):
                pe.wait_ge(v_scaled, n + 1)
                for t in range(GT):
                    for g in range(2):
                        ins = pe.matmul(acc[:, g, 0:P],
                                        kv[:, j % 4, t, 8 * g:8 * g + 8, :],
                                        kv[:, j % 4, t, HEADS + 8 * g:HEADS + 8 * g + 8, :],
                                        start=start and t == 0, stop=stop and t == GT - 1,
                                        skip_group_check=True)
                ins.then_inc(kv_done, 1)

            def project(n, j):
                for t in range(GT):
                    o = prod[:, 2 * (j % 2) + t, 0:KV]
                    pe.matmul(o, ones_rows[:, :], bias_rows[:, :], start=True, stop=False)
                    tok = (j % SPQ) * GT * TILE + t * TILE
                    for a in range(HALVES):
                        hi = y_hi[:, j // SPQ, a, tok:tok + TILE]
                        lo = y_lo[:, j // SPQ, a, tok:tok + TILE]
                        pe.matmul(o, hi, w_hi[:, a, :], start=False, stop=False)
                        pe.matmul(o, hi, w_lo[:, a, :], start=False, stop=False)
                        ins = pe.matmul(o, lo, w_hi[:, a, :], start=False, stop=a == HALVES - 1)
                ins.then_inc(projected, 1)

            def image(b, more):
                pe.wait_ge(added, GRANT + IU * b)

                def body(k, first, last):
                    n0 = (b * BLOCKS + k) * STEPS
                    for j in range(STEPS):
                        if j % SPQ == 0:
                            pe.wait_ge(split_ready, 2 * IQ * b + QUARTERS * k + j // SPQ + 1)
                        if not (first and j < 2):
                            pe.wait_ge(copied, n0 + j - 1)
                        project(n0 + j, j)
                        if not (first and j < 2):
                            accumulate(n0 + j - 2, (j - 2) % STEPS, first and j == 2, False)
                    if last:
                        accumulate(n0 + STEPS - 2, STEPS - 2, False, False)
                        accumulate(n0 + STEPS - 1, STEPS - 1, False, True)
                blocks(pe, body)

                pe.wait_ge(s_ready, b + 1)
                pe.wait_ge(copied, ISTEPS * (b + 1))
                for g in range(2):
                    ins = pe.matmul(prod[:, g, 0:C + 1], s_mat[:, g, :], g_mat[:, g, :], start=True, stop=True)
                ins.then_inc(u_prod, 1)
                pe.wait_ge(u_ready, b + 1)
                for g in range(2):
                    for a in range(HALVES):
                        pe.matmul(prod[:, 2, a * C + g * P:a * C + (g + 1) * P],
                                  u_mat[:, g, a * P:(a + 1) * P], l_mat[:, g, :], start=True, stop=True)
                for g in range(2):
                    ins = pe.matmul(small[:, 8 + g:9 + g], l_mat[:, g, :], u_mat[:, g, C:C + 1], start=True, stop=True)
                ins.then_inc(m_prod, 1)

                with pe.Fori(0, BLOCKS) as k:
                    pe.wait_ge(m_ready, b + 1)
                    for u in range(UNITS):
                        part, half = u // 2, u % 2
                        if half == 0:
                            pe.wait_ge(split_ready, IQ * (2 * b + 1) + QUARTERS * k + QPP * part + QPP)
                        pe.wait_ge(added, IU * b + UNITS * k + u + 1)
                        cols = slice(half * P, (half + 1) * P)
                        for p in range(QPP):
                            q = QPP * part + p
                            o = prod[:, 2 * half + p, :]
                            for a in range(HALVES):
                                pe.matmul(o, m_hi[:, a, cols], y_hi[:, q, a, :], start=a == 0, stop=False)
                                pe.matmul(o, m_hi[:, a, cols], y_lo[:, q, a, :], start=False, stop=False)
                                ins = pe.matmul(o, m_lo[:, a, cols], y_hi[:, q, a, :], start=False,
                                                stop=a == HALVES - 1)
                        ins.then_inc(mixed, 1)
                if more:
                    group_stats(b + 1)

            group_stats(0)
            images(pe, image)


def _tables():
    import numpy as np
    q = np.zeros((D, J))
    for j in range(J):
        q[:j + 1, j] = 1.0 / np.sqrt((j + 1) * (j + 2))
        q[j + 1, j] = -(j + 1) / np.sqrt((j + 1) * (j + 2))
    t = np.zeros((P, C_WIDTH))
    for h in range(2):
        for kind in range(2):
            r = 48 * h + 16 * (1 + kind)
            t[r:r + D, C_HEL + 30 * kind + J * h:C_HEL + 30 * kind + J * (h + 1)] = q
        t[48 * h:48 * h + D, C_QG + 16 * h:C_QG + 16 * h + J] = q
        t[48 * h:48 * h + D, C_EG + 16 * h + J] = 1.0
    for h in range(8):
        s = slice(16 * h, 16 * h + 16)
        t[16 * h:16 * h + J, C_QL + 16 * h:C_QL + 16 * h + 16] = q.T
        t[16 * h + J, C_EL + 16 * h:C_EL + 16 * h + 16] = 1.0
        t[s, C_MASK + 16 * h:C_MASK + 16 * h + 16] = 1.0 / N
    for g in range(P // GROUP):
        t[GROUP * g:GROUP * (g + 1), C_AVG + GROUP * g:C_AVG + GROUP * (g + 1)] = 1.0 / GROUP
    for i in range(3):
        t[i + 1:3, C_E3 + i] = 1.0
    return t.astype(np.float32)


_INS = ["x", "L0_conv_w_qkv", "L0_conv_b_qkv", "L0_conv_kln_w", "L0_conv_kln_b", "L0_conv_vln_w", "L0_conv_vln_b"]


def kernel(**inputs):
    import numpy as _np
    import concourse.bacc as _bacc
    from concourse import mybir as _mybir
    from concourse.bass_utils import run_bass_kernel_spmd as _run

    nc = _bacc.Bacc("TRN2", target_bir_lowering=False, num_devices=1)
    arrays, args = {}, []
    for name in _INS:
        a = _np.ascontiguousarray(inputs[name])
        arrays[f"in_{name}"] = a
        args.append(nc.dram_tensor(f"in_{name}", a.shape, _mybir.dt.from_np(a.dtype), kind="ExternalInput").ap())
    tables = _tables()
    arrays["in_tables"] = tables
    args.append(nc.dram_tensor("in_tables", tables.shape, fp32, kind="ExternalInput").ap())
    args.append(nc.dram_tensor("out_0", (B, C, H, W), fp32, kind="ExternalOutput").ap())
    build(nc, *args)
    r = _run(nc, [arrays], core_ids=[0])
    return r.results[0]["out_0"]
```

```python
from contextlib import ExitStack

import concourse.bass as bass
from concourse import mybir

B, C, H, W = 8, 256, 128, 128
N = H * W
HEADS, D = 16, 16
J = D - 1
P = 128
HALVES = C // P
NG = 32
GROUP = C // NG
PAIR = 2 * 3 * D
PAIRS = HEADS // 2
GN_EPS, LN_EPS = 1e-5, 1e-5

SLOT = 1024
ISLOTS = N // SLOT
SLOTS = ISLOTS + 3
BLOCK = 2048
PARTS = BLOCK // SLOT
BLOCKS = N // BLOCK
QTOK = 512
QUARTERS = BLOCK // QTOK
QPP = QUARTERS // PARTS
IQ = QUARTERS * BLOCKS
TILE = 128
GT = 2
STEPS = BLOCK // (TILE * GT)
SPQ = STEPS // QUARTERS
STOK = TILE * GT
FIRST = 3
LEAD = 4
ISTEPS = STEPS * BLOCKS
KV = 2 * HEADS * J
UNITS = 2 * PARTS
IU = UNITS * BLOCKS
IMAGE_OWN = 10
GRANT = 2
IDLE = (9, 7, 3, 10)
Y_SCALE = 64.0
W_SCALE = 1024.0
M_SCALE = 1024.0
TINY = 1e-30

C_MASK, C_AVG, C_KEPT = 0, 128, 256
C_HEL, C_QG, C_EG, C_QL, C_EL = 256, 316, 348, 380, 508
C_WIDTH = 636

fp32 = mybir.dt.float32
fp16 = mybir.dt.float16
ALU = mybir.AluOpType
ACT = mybir.ActivationFunctionType
AX = mybir.AxisListType
RMAX = bass.bass_isa.ReduceOp.max


def build(nc, x, w_qkv, b_qkv, kln_w, kln_b, vln_w, vln_b, consts, out):
    x_v = x.rearrange("b (a p) h w -> b p a (h w)", p=P)
    out_v = out.rearrange("b (a p) h w -> b p a (h w)", p=P)

    ctx = ExitStack()
    with ctx:
        def sb(name, shape, dt):
            return ctx.enter_context(nc.sbuf_tensor(name, shape, dt))

        def sem(name):
            return ctx.enter_context(nc.semaphore(name))

        ring = sb("ring", [P, SLOTS, HALVES, SLOT], fp32)
        y_hi = sb("y_hi", [P, QUARTERS, HALVES, QTOK], fp16)
        y_lo = sb("y_lo", [P, QUARTERS, HALVES, QTOK], fp16)
        kv = sb("kv", [P, 4, GT, 2 * HEADS, D], fp32)
        scratch = sb("scratch", [P, 2, SLOT], fp32)
        sigma = sb("sigma", [P, 4, GT, 2 * HEADS], fp32)
        sig_kv = sb("sig_kv", [P, 4, GT, HEADS], fp32)
        inv_kv = sb("inv_kv", [P, 4, GT, HEADS], fp32)
        w_hi = sb("w_hi", [P, HALVES, KV], fp16)
        w_lo = sb("w_lo", [P, HALVES, KV], fp16)
        bias = sb("bias", [P, KV], fp32)
        eps_h = sb("eps_h", [P, 2 * HEADS], fp32)
        tab = sb("tab", [P, C_KEPT], fp32)
        g_mat = sb("g_mat", [P, 2, C + 1], fp32)
        l_mat = sb("l_mat", [P, 2, P], fp32)
        kv_flat = kv[:, :, :, :, :].rearrange("p i t h j -> p (i t h j)")
        s_mat = kv_flat[:, 0:2 * P].rearrange("p (g n) -> p g n", g=2)
        u_mat = kv_flat[:, 1024:1024 + 2 * (C + 1)].rearrange("p (g n) -> p g n", g=2)
        stage = kv_flat.rearrange("p (u n) -> p u n", u=UNITS)
        m_hi = sb("m_hi", [P, HALVES, C], fp16)
        m_lo = sb("m_lo", [P, HALVES, C], fp16)
        gl_max = sb("gl_max", [P, 4], fp32)
        gl_scale = sb("gl_scale", [P, 4], fp32)
        gl_inv = sb("gl_inv", [P, 4], fp32)
        row_scale = sb("row_scale", [P, 2], fp32)
        out_scale = sb("out_scale", [P, 2], fp32)
        shift = sb("shift", [P, HALVES], fp32)
        stats = sb("stats", [P, HALVES, N // 512, 6], fp32)
        chan = sb("chan", [P, HALVES, 2], fp32)
        dev = sb("dev", [P, HALVES], fp32)
        dev2 = sb("dev2", [P, HALVES], fp32)
        gmean = sb("gmean", [P, HALVES], fp32)
        gn_eps = sb("gn_eps", [P, 1], fp32)
        y_scale = sb("y_scale", [P, HALVES], fp32)
        y_shift = sb("y_shift", [P, HALVES], fp32)
        x_scale = sb("x_scale", [P, HALVES], fp32)

        room = ring[:, SLOTS - 2:SLOTS, :, :].rearrange("p s a n -> p (s a n)")
        at = [0]

        def setup_room(rows, width):
            at[0] += width
            assert at[0] <= 2 * HALVES * SLOT
            return room[0:rows, at[0] - width:at[0]]

        tab2 = setup_room(P, C_WIDTH - C_KEPT)
        wt = setup_room(PAIR, PAIRS * (C + 1)).rearrange("p (t n) -> p t n", t=PAIRS)
        ones = setup_room(1, P)
        brow = setup_room(1, KV)
        klw = setup_room(PAIR, PAIRS)
        klb = setup_room(PAIR, PAIRS)
        lk = setup_room(PAIR, PAIRS * 32).rearrange("p (t n) -> p t n", t=PAIRS)
        vlw = setup_room(P, C)
        vlb = setup_room(P, C)
        wmax = setup_room(P, 3 * 32).rearrange("p (a n) -> p a n", a=3)
        amax = setup_room(P, 32)
        alpha = setup_room(P, 32)
        w0 = C_WIDTH - C_KEPT
        ws = room[:, w0:w0 + KV]

        prod = ctx.enter_context(nc.psum_tensor("prod", [P, 4, 512], fp32))
        acc = ctx.enter_context(nc.psum_tensor("acc", [P, 2, 512], fp32))
        unread = ctx.enter_context(nc.psum_tensor("unread", [P, 512], fp32))
        small = ctx.enter_context(nc.psum_tensor("small", [P, 512], fp32))

        hel = tab2[0:PAIR, C_HEL - C_KEPT:C_HEL - C_KEPT + 60].rearrange("p (v x) -> p v x", v=2)
        avg = tab[:, C_AVG:C_AVG + P]
        mask = tab[:, C_MASK:C_MASK + P]

        consts_in = sem("consts_in")
        setup_cleared = sem("setup_cleared")
        setup_w = sem("setup_w")
        setup_g = sem("setup_g")
        setup_lk = sem("setup_lk")
        setup_amax = sem("setup_amax")
        setup_wmax = sem("setup_wmax")
        setup_brow = sem("setup_brow")
        setup_rows = sem("setup_rows")
        setup_scale = sem("setup_scale")
        setup_done = sem("setup_done")
        first_in = [sem(f"first_in{i}") for i in range(ISLOTS)]
        refill_in = [sem(f"refill_in_{u}") for u in range(UNITS)]
        stored = [sem(f"stored_{u}") for u in range(UNITS)]
        chan_ready = sem("chan_ready")
        group_sum = sem("group_sum")
        std_ready = sem("std_ready")
        normed_first = sem("normed_first")
        normed = sem("normed")
        hi_ready = sem("hi_ready")
        split_ready = sem("split_ready")
        half_read = sem("half_read")
        projected = sem("projected")
        squared = sem("squared")
        biased = sem("biased")
        summed = sem("summed")
        sigma_ready = sem("sigma_ready")
        sig_kv_ready = sem("sig_kv_ready")
        v_scaled = sem("v_scaled")
        kv_done = sem("kv_done")
        s_ready = sem("s_ready")
        u_prod = sem("u_prod")
        u_ready = sem("u_ready")
        m_prod = sem("m_prod")
        m_ready = sem("m_ready")
        shift_ready = sem("shift_ready")
        mixed = sem("mixed")
        shifted = sem("shifted")
        added = sem("added")
        pool_sig = sem("pool_sig")
        act_setup = sem("act_setup")
        inv_ready = sem("inv_ready")
        stats_done = sem("stats_done")
        carried = {e.engine: sem(f"carried_{n}") for n, e in
                   (("sp", nc.sync), ("act", nc.scalar), ("pool", nc.gpsimd), ("dve", nc.vector))}
        dve_step = sem("dve_step")

        block = ctx.enter_context(nc.Block())

        def slot(i):
            return ring[:, i % SLOTS:i % SLOTS + 1, :, :] if isinstance(i, int) else \
                ring[:, bass.ds(i % SLOTS, 1), :, :]

        def quarter(b, k, q):
            tok = (q % QPP) * QTOK
            return slot((b * BLOCKS + k) * PARTS + q // QPP)[:, :, :, tok:tok + QTOK]

        def step_of(b, k, j):
            tok = (j * STOK) % SLOT
            return slot((b * BLOCKS + k) * PARTS + j * STOK // SLOT)[:, :, :, tok:tok + STOK]

        def staged(t, j):
            tok = (j % SPQ) * STOK
            return t[:, j // SPQ:j // SPQ + 1, :, tok:tok + STOK]

        def settled(eng):
            eng.sem_inc(carried[eng.engine], 1)

        def images(eng, body):
            with eng.Fori(0, B - 1) as b:
                body(b, True)
            body(B - 1, False)

        def blocks(eng, body):
            body(0, True, False)
            with eng.Fori(1, BLOCKS - 1) as k:
                body(k, False, False)
            body(BLOCKS - 1, False, True)

        @block.sync
        def _(sp):
            sp.wait_ge(consts_in, 16 * 10)
            for i in range(ISLOTS):
                sp.dma_start(ring[:, i, :, :], x_v[0, :, :, i * SLOT:(i + 1) * SLOT]).then_inc(first_in[i], 16)
            for i in range(ISLOTS, SLOTS):
                part = (i - SLOTS) % PARTS
                for half in range(HALVES):
                    loaded = refill_in[2 * part + half]
                    if i == ISLOTS + 1 and half == 0:
                        sp.wait_ge(setup_done, 1)
                    if i >= ISLOTS + PARTS:
                        sp.wait_ge(loaded, 16)
                    sp.dma_start(ring[:, i, half, :], x_v[1, :, half, (i - ISLOTS) * SLOT:(i - ISLOTS + 1) * SLOT])\
                      .then_inc(loaded, 16)

            ring_flat = ring[:, :, :, :].rearrange("p s a n -> p (s a n)")

            def slot_at(i, half):
                return ring_flat[:, bass.ds((i % SLOTS) * (HALVES * SLOT) + half * SLOT, SLOT)]

            def tokens_at(t, i, half):
                o = (i // ISLOTS) * (C * N) + (i % ISLOTS) * SLOT + half * (P * N)
                return bass.AP(tensor=t.tensor, offset=o, ap=[[N, P], [1, SLOT]])

            def refill(kk, u):
                sp.wait_ge(refill_in[u], 16 * (kk + 1 + u // 2))
                settled(sp)
                i = kk * PARTS + u // 2 + SLOTS
                sp.dma_start(slot_at(i, u % 2), tokens_at(x, i, u % 2)).then_inc(refill_in[u], 16)

            def staged_block(b, k, refills):
                kk = b * BLOCKS + k
                for u in range(UNITS):
                    sp.wait_ge(added, GRANT + IU * b + UNITS * k + u + 1)
                    settled(sp)
                    if u < refills:
                        refill(kk, u)
                    sp.dma_start(tokens_at(out, kk * PARTS + u // 2, u % 2), stage[:, u, :]).then_inc(stored[u], 16)

            def last_block(b, refills):
                kk = b * BLOCKS + BLOCKS - 1
                for u in range(UNITS):
                    sp.wait_ge(stored[u], 16 * kk)
                    if not isinstance(kk, int):
                        settled(sp)
                    sp.wait_ge(added, GRANT + IU * b + UNITS * (BLOCKS - 1) + u + 1)
                    if not isinstance(kk, int):
                        settled(sp)
                    i = kk * PARTS + u // 2
                    sp.dma_start(tokens_at(out, i, u % 2), slot_at(i, u % 2)).then_inc(stored[u], 16)
                for u in range(UNITS):
                    sp.wait_ge(stored[u], 16 * (kk + 1))
                    if not isinstance(kk, int):
                        settled(sp)
                    if u < refills:
                        refill(kk, u)

            with sp.Fori(0, B - 2) as b:
                with sp.Fori(0, BLOCKS - 1) as k:
                    staged_block(b, k, UNITS)
                last_block(b, UNITS)
            for b, loads in ((B - 2, ISLOTS - (SLOTS - ISLOTS)), (B - 1, 0)):
                full = loads // PARTS
                if full:
                    with sp.Fori(0, full) as k:
                        staged_block(b, k, UNITS)
                for k in range(full, full + 1 if loads % PARTS else full):
                    staged_block(b, k, UNITS // PARTS * (loads % PARTS))
                done = (loads + PARTS - 1) // PARTS
                if done < BLOCKS - 1:
                    with sp.Fori(done, BLOCKS - 1) as k:
                        staged_block(b, k, 0)
                last_block(b, 0)

        @block.gpsimd
        def _(pool):
            nc.gpsimd.memset(klw, 0.0)
            nc.gpsimd.memset(klb, 0.0).then_inc(setup_cleared, 1)
            pool.wait_ge(setup_wmax, 1)
            nc.gpsimd.partition_all_reduce(amax, wmax[:, 0, :], P, RMAX).then_inc(setup_amax, 1)

            def lows(b, k, j):
                pool.wait_ge(hi_ready, 2 * ISTEPS * b + STEPS * k + j + 1)
                settled(pool)
                nc.gpsimd.tensor_tensor(staged(y_lo, j), step_of(b, k, j), staged(y_hi, j),
                                        ALU.subtract).then_inc(split_ready, 1)

            def lows_again(b, k, q):
                pool.wait_ge(hi_ready, ISTEPS * (2 * b + 1) + STEPS * k + SPQ * (q + 1))
                settled(pool)
                nc.gpsimd.tensor_tensor(y_lo[:, q:q + 1, :, :], quarter(b, k, q),
                                        y_hi[:, q:q + 1, :, :], ALU.subtract).then_inc(split_ready, SPQ)

            def scale_v(m, j):
                pool.wait_ge(inv_ready, m + 1)
                v = kv[:, j % 4, :, HEADS:, 0:J]
                nc.gpsimd.tensor_tensor(v, v, inv_kv[:, j % 4, :, :, None].to_broadcast([P, GT, HEADS, J]),
                                        ALU.mult).then_inc(v_scaled, 1)

            def sigmas(n, m, j):
                pool.wait_ge(sigma_ready, n + 1)
                s16 = kv[:, j % 4, :, :, J]
                nc.gpsimd.tensor_tensor(s16, sigma[:, j % 4, :, :],
                                        eps_h[:, None, :].to_broadcast([P, GT, 2 * HEADS]),
                                        ALU.add).then_inc(pool_sig, 1)
                pool.wait_ge(pool_sig, m + 1)
                nc.gpsimd.tensor_tensor(sig_kv[:, j % 4, :, :], kv[:, j % 4, :, 0:HEADS, J],
                                        kv[:, j % 4, :, HEADS:, J], ALU.mult).then_inc(sig_kv_ready, 1)

            def image(b, more):
                for j in range(LEAD):
                    lows(b, 0, j)

                def body(k, first, last):
                    n0 = (b * BLOCKS + k) * STEPS
                    m0 = b * (ISTEPS - 1) + k * STEPS
                    for j in range(STEPS):
                        if not (first and j < 2):
                            scale_v(m0 + j - 2, (j - 2) % STEPS)
                        if not (first and j < 1):
                            sigmas(n0 + j - 1, m0 + j - 1, (j - 1) % STEPS)
                        if j + LEAD < STEPS:
                            lows(b, k, j + LEAD)
                        elif not last:
                            lows(b, k + 1, j + LEAD - STEPS)
                    if last:
                        scale_v(m0 + STEPS - 2, STEPS - 2)
                blocks(pool, body)

                for q in range(QPP):
                    lows_again(b, 0, q)
                with pool.Fori(0, BLOCKS - 1) as k:
                    for q in range(QUARTERS):
                        if q + QPP < QUARTERS:
                            lows_again(b, k, q + QPP)
                        else:
                            lows_again(b, k + 1, q + QPP - QUARTERS)
                for q in range(QPP, QUARTERS):
                    lows_again(b, BLOCKS - 1, q)

            images(pool, image)

        @block.scalar
        def _(act):
            act.dma_start(tab[:, :], consts[:, 0:C_KEPT]).then_inc(consts_in, 16)
            act.dma_start(tab2, consts[:, C_KEPT:]).then_inc(consts_in, 16)
            with nc.allow_non_contiguous_dma(reason="small parameters"):
                act.dma_start(wt[:, :, 0:C], w_qkv.rearrange("(t p) c -> p t c", p=PAIR)).then_inc(consts_in, 16)
                act.dma_start(wt[:, :, C:C + 1], b_qkv.rearrange("(t p one) -> p t one", p=PAIR, one=1)).then_inc(consts_in, 16)
                act.dma_start(vlw, vln_w.rearrange("(one h) d -> one (h d)", one=1).to_broadcast([P, C])).then_inc(consts_in, 16)
                act.dma_start(vlb, vln_b.rearrange("(one h) d -> one (h d)", one=1).to_broadcast([P, C])).then_inc(consts_in, 16)
                act.wait_ge(setup_cleared, 1)
                for row in range(2):
                    q0 = row * 3 * D
                    act.dma_start(klw[q0:q0 + D, :], kln_w.rearrange("(t r) d -> r d t", r=2)[row]).then_inc(consts_in, 16)
                    act.dma_start(klb[q0:q0 + D, :], kln_b.rearrange("(t r) d -> r d t", r=2)[row]).then_inc(consts_in, 16)

            act.wait_ge(setup_g, 1)
            nc.scalar.activation(g_mat[:, 0, :], acc[:, 0, 0:C + 1], ACT.Copy).then_inc(act_setup, 1)
            nc.scalar.activation(g_mat[:, 1, :], acc[:, 1, 0:C + 1], ACT.Copy).then_inc(act_setup, 1)

            def group_std(b):
                act.wait_ge(group_sum, 2 * b + 2)
                nc.scalar.activation(x_scale[:, :], small[:, 0:HALVES], ACT.Sqrt, scale=1.0 / Y_SCALE ** 2,
                                     bias=gn_eps[:, 0:1])\
                  .then_inc(std_ready, 1)

            def normalise(b, k, q):
                v = quarter(b, k, q)
                for a in range(HALVES):
                    ins = nc.scalar.activation(v[:, :, a, :], v[:, :, a, :], ACT.Identity,
                                               scale=y_scale[:, a:a + 1], bias=y_shift[:, a:a + 1])
                ins.then_inc(normed, 1)

            def highs(b, k, j, first):
                q = j // SPQ
                if first and q < FIRST:
                    act.wait_ge(normed_first, SPQ * (FIRST * b + q) + (j + 1 if q == 0 else SPQ))
                else:
                    act.wait_ge(normed, (IQ - FIRST) * b + QUARTERS * k + q - FIRST + 1)
                if not first:
                    act.wait_ge(projected, ISTEPS * b + STEPS * k + j - STEPS + 1)
                settled(act)
                nc.scalar.activation(staged(y_hi, j), step_of(b, k, j), ACT.Copy).then_inc(hi_ready, 1)

            def highs_again(b, k, q, first):
                if first:
                    act.wait_ge(projected, SPQ * (IQ * b + IQ - QUARTERS + q + 1))
                elif q % QPP == 0:
                    act.wait_ge(half_read, PARTS * (BLOCKS * b + k - 1) + q // QPP + 1)
                else:
                    act.wait_ge(mixed, IU * b + UNITS * (k - 1) + 2 * (q // QPP) + 2)
                settled(act)
                nc.scalar.activation(y_hi[:, q:q + 1, :, :], quarter(b, k, q), ACT.Copy).then_inc(hi_ready, SPQ)

            def squares(n, j, waits):
                act.wait_ge(biased, n + 1)
                if waits:
                    act.wait_ge(summed, n - 1)
                nc.scalar.activation(
                    scratch[:, j % 2, 0:GT * KV].rearrange("p (t h j) -> p t h j", t=GT, j=J),
                    kv[:, j % 4, :, :, 0:J], ACT.Square).then_inc(squared, 1)

            def roots(n, j):
                act.wait_ge(summed, n + 1)
                nc.scalar.activation(sigma[:, j % 4, :, :], sigma[:, j % 4, :, :], ACT.Sqrt,
                                     scale=1.0 / (D - 1)).then_inc(sigma_ready, 1)

            def image(b, more):
                for j in range(LEAD):
                    highs(b, 0, j, True)

                def body(k, first, last):
                    n0 = (b * BLOCKS + k) * STEPS
                    for j in range(STEPS):
                        squares(n0 + j, j, not (first and j < 2))
                        if not (first and j < 1):
                            roots(n0 + j - 1, (j - 1) % STEPS)
                        if j + LEAD < STEPS:
                            highs(b, k, j + LEAD, first)
                        elif not last:
                            highs(b, k + 1, j + LEAD - STEPS, False)
                        if j % SPQ == 0:
                            q = j // SPQ + FIRST
                            if q < QUARTERS:
                                normalise(b, k, q)
                            elif not last:
                                normalise(b, k + 1, q - QUARTERS)
                    if last:
                        roots(n0 + STEPS - 1, STEPS - 1)
                blocks(act, body)

                for q in range(QPP):
                    highs_again(b, 0, q, True)

                for g in range(2):
                    act.wait_ge(u_prod, 2 * b + g + 1)
                    nc.scalar.activation(u_mat[:, g, :], prod[:, g, 0:C + 1], ACT.Copy).then_inc(u_ready, 1)

                def body_b(k, first, last):
                    for u in range(UNITS):
                        n = IU * b + UNITS * k + u
                        part, half = u // 2, u % 2
                        q = QPP * part + QPP + half
                        if q < QUARTERS:
                            highs_again(b, k, q, first)
                        elif not last:
                            highs_again(b, k + 1, q - QUARTERS, False)
                        if first and u == 0:
                            act.wait_ge(shift_ready, b + 1)
                        act.wait_ge(added, n + 1)
                        settled(act)
                        nc.scalar.activation(
                            scratch[:, half:half + 1, :], slot((b * BLOCKS + k) * PARTS + part)[:, :, half, :],
                            ACT.Identity, scale=x_scale[:, half:half + 1],
                            bias=shift[:, half:half + 1]).then_inc(shifted, 1)
                blocks(act, body_b)
                if more:
                    act.wait_ge(shifted, IU * (b + 1))
                    group_std(b + 1)

            group_std(0)
            images(act, image)

        @block.vector
        def _(dve):
            count = [0, 0]

            def own(ins):
                count[1] += 1
                ins.then_inc(dve_step, 1)
                dve.wait_ge(dve_step, count[0] + count[1])

            def half_stats(i, at, half):
                for h in range(SLOT // 512):
                    o = stats[:, half, 2 * at + h, :] if isinstance(at, int) else \
                        stats[:, half, bass.ds(2 * at + h, 1), :]
                    v = slot(i)[:, 0, half, h * 512:(h + 1) * 512] if isinstance(i, int) else \
                        slot(i)[:, :, half, h * 512:(h + 1) * 512]
                    dve.bn_stats(o, v).then_inc(stats_done, 1)

            def early_stats(b, m):
                at, tok, half = m // 4, m // 2, m % 2
                i = (b + 1) * ISLOTS + at
                slots = ring[:, :, :, :].rearrange("p s a n -> p (s a n)")
                st = stats[:, :, :, :].rearrange("p a t v -> p (a t v)")
                dve.bn_stats(st[:, bass.ds((half * (N // 512) + tok) * 6, 6)],
                             slots[:, bass.ds(((i % SLOTS) * HALVES + half) * SLOT + (tok % 2) * 512, 512)])\
                   .then_inc(stats_done, 1)

            def first_stats(slots):
                for i in slots:
                    dve.wait_ge(first_in[i], 16)
                    for half in range(HALVES):
                        half_stats(i, i, half)

            dve.memset(ones, 1.0)
            dve.wait_ge(consts_in, 16 * 10)
            qg = tab2[0:PAIR, C_QG - C_KEPT:C_QG - C_KEPT + 32]
            eg = tab2[0:PAIR, C_EG - C_KEPT:C_EG - C_KEPT + 32]
            for t in range(PAIRS):
                own(dve.tensor_scalar(lk[:, t, :], qg, klw[:, t:t + 1], None, ALU.mult))
            for t in range(PAIRS):
                ins = dve.scalar_tensor_tensor(lk[:, t, :], eg, klb[:, t:t + 1], lk[:, t, :], ALU.mult, ALU.add)
            ins.then_inc(setup_lk, 1)
            for g in range(2):
                w_g, b_g = vlw[:, g * P:(g + 1) * P], vlb[:, g * P:(g + 1) * P]
                own(dve.tensor_tensor(l_mat[:, g, :], tab2[:, C_QL - C_KEPT:C_QL - C_KEPT + P], w_g, ALU.mult))
                own(dve.tensor_tensor(b_g, tab2[:, C_EL - C_KEPT:C_EL - C_KEPT + P], b_g, ALU.mult))
                own(dve.tensor_tensor(l_mat[:, g, :], l_mat[:, g, :], b_g, ALU.add))
            first_stats(range(0, 3))
            dve.wait_ge(setup_w, 1)
            dve.tensor_copy(brow, prod[0:1, 2, 0:KV]).then_inc(setup_brow, 1)
            first_stats(range(3, 4))
            dve.wait_ge(setup_w, 2)
            for i, bank in enumerate((0, 1, 3)):
                own(dve.tensor_reduce(wmax[:, i, :], prod[:, bank, 0:KV].rearrange("p (h j) -> p h j", j=J),
                                      AX.X, ALU.max, apply_absolute_value=True))
            own(dve.tensor_tensor(wmax[:, 0, :], wmax[:, 0, :], wmax[:, 1, :], ALU.max))
            dve.tensor_tensor(wmax[:, 0, :], wmax[:, 0, :], wmax[:, 2, :], ALU.max).then_inc(setup_wmax, 1)
            dve.wait_ge(act_setup, 2)
            own(dve.tensor_reduce(gl_max[:, 0:2], g_mat[:, :, 0:C], AX.X, ALU.max, apply_absolute_value=True))
            dve.tensor_reduce(gl_max[:, 2:4], l_mat[:, :, :], AX.X, ALU.max, apply_absolute_value=True).then_inc(setup_rows, 1)
            first_stats(range(4, 6))
            dve.wait_ge(setup_scale, 1)
            own(dve.tensor_scalar(gl_scale[:, :], small[:, 0:4], float(N), TINY, ALU.mult, ALU.max))
            own(dve.reciprocal(gl_inv[:, :], gl_scale[:, :]))
            for g in range(2):
                own(dve.tensor_scalar(g_mat[:, g, :], g_mat[:, g, :], gl_inv[:, g:g + 1], None, ALU.mult))
                own(dve.tensor_scalar(l_mat[:, g, :], l_mat[:, g, :], gl_inv[:, 2 + g:3 + g], None, ALU.mult))
            own(dve.tensor_tensor(row_scale[:, :], gl_scale[:, 0:2], gl_scale[:, 2:4], ALU.mult))
            own(dve.tensor_scalar(out_scale[:, :], row_scale[:, :], 1.0 / (M_SCALE * Y_SCALE), None, ALU.mult))
            dve.wait_ge(setup_amax, 1)
            own(dve.tensor_scalar(amax, amax, TINY, None, ALU.max))
            own(dve.reciprocal(alpha, amax))
            own(dve.tensor_scalar(eps_h[:, :], alpha, LN_EPS * W_SCALE * Y_SCALE, None, ALU.mult))
            own(dve.tensor_scalar(alpha, alpha, W_SCALE, None, ALU.mult))
            heads = alpha[:, :, None].to_broadcast([P, 2 * HEADS, J])
            for a in range(HALVES):
                own(dve.tensor_tensor(ws.rearrange("p (h j) -> p h j", j=J),
                                      prod[:, a, 0:KV].rearrange("p (h j) -> p h j", j=J), heads, ALU.mult))
                own(dve.tensor_copy(w_hi[:, a, :], ws))
                own(dve.tensor_tensor(w_lo[:, a, :], ws, w_hi[:, a, :], ALU.subtract))
            own(dve.tensor_tensor(ws.rearrange("p (h j) -> p h j", j=J),
                                  prod[:, 3, 0:KV].rearrange("p (h j) -> p h j", j=J), heads, ALU.mult))
            own(dve.tensor_scalar(bias[:, :], ws, Y_SCALE, None, ALU.mult))
            dve.tensor_copy(gmean[:, :], tab[:, 0:HALVES]).then_inc(added, GRANT)
            dve.memset(gn_eps[:, :], GN_EPS / Y_SCALE ** 2).then_inc(setup_done, 1)

            def channel_stats(b):
                dve.wait_ge(stats_done, 64 * (b + 1))
                dve.memset(dev[:, :], 0.0)
                for a in range(HALVES):
                    ins = dve.bn_aggr(chan[:, a, :], stats[:, a, :, :])
                ins.then_inc(chan_ready, 1)

            def group_mean():
                own(dve.tensor_copy(gmean[:, :], small[:, 0:HALVES]))
                own(dve.tensor_tensor(dev[:, :], chan[:, :, 0], gmean[:, :], ALU.subtract))
                own(dve.tensor_tensor(dev2[:, :], dev[:, :], dev[:, :], ALU.mult))
                dve.tensor_tensor(dev[:, :], dev2[:, :], chan[:, :, 1], ALU.add).then_inc(chan_ready, 1)

            def group_scale(b):
                dve.wait_ge(std_ready, b + 1)
                own(dve.reciprocal(y_scale[:, :], x_scale[:, :]))
                dve.scalar_tensor_tensor(y_shift[:, :], gmean[:, :], -1.0, y_scale[:, :], ALU.mult, ALU.mult)

            def normalise(b, k, q):
                for a in range(HALVES):
                    v = quarter(b, k, q)[:, :, a, :]
                    ins = dve.tensor_scalar(v, v, gmean[:, a:a + 1], y_scale[:, a:a + 1],
                                            ALU.subtract, ALU.mult)
                ins.then_inc(normed_first, SPQ)

            def normalise_step(b, j):
                for a in range(HALVES):
                    v = step_of(b, 0, j)[:, :, a, :]
                    ins = dve.tensor_scalar(v, v, gmean[:, a:a + 1], y_scale[:, a:a + 1],
                                            ALU.subtract, ALU.mult)
                ins.then_inc(normed_first, 1)

            def sum_squares(n, j):
                dve.wait_ge(squared, n + 1)
                dve.tensor_reduce(sigma[:, j % 4, :, :],
                                  scratch[:, j % 2, 0:GT * KV].rearrange("p (t h j) -> p t h j", t=GT, j=J),
                                  AX.X, ALU.add).then_inc(summed, 1)

            def add_bias(n, j, waits):
                if waits:
                    dve.wait_ge(kv_done, n - 3)
                dve.wait_ge(projected, n + 1)
                dve.tensor_tensor(
                    kv[:, j % 4, :, :, 0:J],
                    prod[:, 2 * (j % 2):2 * (j % 2) + 2, 0:KV].rearrange("p t (h j) -> p t h j", j=J),
                    bias[:, :].rearrange("p (h j) -> p h j", j=J)[:, None, :, :].to_broadcast([P, GT, 2 * HEADS, J]),
                    ALU.add).then_inc(biased, 1)

            def invert(m, j):
                dve.wait_ge(sig_kv_ready, m + 1)
                dve.reciprocal(kv[:, j % 4, :, HEADS:, J], kv[:, j % 4, :, 0:HEADS, J])
                dve.reciprocal(inv_kv[:, j % 4, :, :], sig_kv[:, j % 4, :, :]).then_inc(inv_ready, 1)

            def last_step(b, n, j):
                dve.wait_ge(sigma_ready, n + 1)
                kv_j = kv[:, j % 4, :, :, :]
                own(dve.tensor_tensor(kv_j[:, :, :, J], sigma[:, j % 4, :, :],
                                      eps_h[:, None, :].to_broadcast([P, GT, 2 * HEADS]), ALU.add))
                own(dve.tensor_tensor(sig_kv[:, j % 4, :, :], kv_j[:, :, 0:HEADS, J], kv_j[:, :, HEADS:, J], ALU.mult))
                dve.reciprocal(kv_j[:, :, HEADS:, J], kv_j[:, :, 0:HEADS, J])
                own(dve.reciprocal(inv_kv[:, j % 4, :, :], sig_kv[:, j % 4, :, :]))
                dve.wait_ge(v_scaled, n)
                v = kv_j[:, :, HEADS:, 0:J]
                dve.tensor_tensor(v, v, inv_kv[:, j % 4, :, :, None].to_broadcast([P, GT, HEADS, J]), ALU.mult)\
                   .then_inc(v_scaled, 1)

            first_stats(range(6, ISLOTS))
            channel_stats(0)
            dve.wait_ge(group_sum, 1)
            group_mean()
            group_scale(0)
            for j in range(SPQ):
                normalise_step(0, j)
            for q in range(1, FIRST):
                normalise(0, 0, q)
            setup_steps = count[1]

            def image(b, more):
                count[0], count[1] = b * IMAGE_OWN + setup_steps, 0
                def body(k, first, last):
                    n0 = (b * BLOCKS + k) * STEPS
                    m0 = b * (ISTEPS - 1) + k * STEPS
                    for j in range(STEPS):
                        n = n0 + j
                        add_bias(n, j, not (first and j < 4))
                        if not (first and j < 2):
                            invert(m0 + j - 2, (j - 2) % STEPS)
                        if not (first and j < 1):
                            sum_squares(n - 1, (j - 1) % STEPS)
                        if more and first and j == STEPS // 2:
                            for u in range(UNITS):
                                dve.wait_ge(refill_in[u], 16 * (b * BLOCKS + 1))
                        if more and not first and not last and j == 3:
                            early_stats(b, k - 1)
                        if more and last and j in (3, 5):
                            early_stats(b, BLOCKS - 2 + j // 4)
                    if last:
                        sum_squares(n0 + STEPS - 1, STEPS - 1)
                        invert(m0 + STEPS - 2, STEPS - 2)
                        last_step(b, n0 + STEPS - 1, STEPS - 1)
                blocks(dve, body)

                dve.wait_ge(kv_done, ISTEPS * (b + 1))
                dve.tensor_tensor(s_mat, acc[:, :, 0:P],
                                  mask[:, None, :].to_broadcast([P, 2, P]), ALU.mult).then_inc(s_ready, 1)
                for g in range(2):
                    dve.wait_ge(m_prod, 3 * b + g + 1)
                    m_psum = prod[:, 2 + g, 0:C].rearrange("p (a c) -> p a c", a=HALVES)
                    m_cols = slice(g * P, (g + 1) * P)
                    own(dve.tensor_scalar(m_hi[:, :, m_cols], m_psum, M_SCALE, None, ALU.mult))
                    dve.scalar_tensor_tensor(m_lo[:, :, m_cols], m_psum, M_SCALE, m_hi[:, :, m_cols],
                                             ALU.mult, ALU.subtract).then_inc(m_ready, 1)
                dve.wait_ge(m_prod, 3 * b + 3)
                own(dve.tensor_tensor(shift[:, :], small[:, 8:8 + HALVES], row_scale[:, :], ALU.mult))
                dve.tensor_tensor(shift[:, :], shift[:, :], gmean[:, :], ALU.add).then_inc(shift_ready, 1)

                def body_b(k, first, last):
                    for u in range(UNITS):
                        n = IU * b + UNITS * k + u
                        part, half = u // 2, u % 2
                        at = k * PARTS + part
                        end = last and part == PARTS - 1
                        if more and end and half == 0:
                            channel_stats(b + 1)
                            dve.wait_ge(group_sum, 2 * (b + 1) + 1)
                            group_mean()
                        if more and end and half == 1:
                            group_scale(b + 1)
                            normalise_step(b + 1, 0)
                        dve.wait_ge(shifted, n + 1)
                        dve.wait_ge(mixed, n + 1)
                        if not first and not last:
                            dve.wait_ge(stored[u], 16 * (b * BLOCKS + k))
                        o = slot(b * ISLOTS + at)[:, :, half, :] if last else stage[:, u:u + 1, :]
                        dve.scalar_tensor_tensor(
                            o.rearrange("p s (t n) -> p (s t) n", t=2),
                            prod[:, 2 * half:2 * half + 2, :], out_scale[:, half:half + 1],
                            scratch[:, half, :].rearrange("p (t n) -> p t n", t=2),
                            ALU.mult, ALU.add).then_inc(added, 1)
                        if more and not (first and part == 0) and not end:
                            dve.wait_ge(refill_in[u], 16 * (b * BLOCKS + k + 1 + part))
                            half_stats((b + 1) * ISLOTS + at + 1, at + 1, half)
                blocks(dve, body_b)
                if more:
                    normalise_step(b + 1, 1)
                    for q in range(1, FIRST):
                        normalise(b + 1, 0, q)
                    for u in range(UNITS):
                        dve.wait_ge(stored[u], 16 * (b * BLOCKS + BLOCKS - 1))
                    settled(dve)
                    assert count[1] == IMAGE_OWN

            images(dve, image)

        @block.tensor
        def _(pe):
            pe.wait_ge(consts_in, 16 * 10)
            pe.wait_ge(setup_lk, 1)
            for t in range(PAIRS):
                for a in range(HALVES):
                    o = prod[:, a, 0:KV].rearrange("p (v x) -> p v x", v=2)[:, :, 30 * t:30 * t + 30]
                    pe.matmul(o, wt[:, t, a * P:(a + 1) * P], hel, start=True, stop=True)
                o = prod[0:1, 2, 0:KV].rearrange("p (v x) -> p v x", v=2)[:, :, 30 * t:30 * t + 30]
                ins = pe.matmul(o, wt[:, t, C:C + 1], hel, start=True, stop=True)
            ins.then_inc(setup_w, 1)
            for t in range(PAIRS):
                r = 32 * (t % 4)
                ins = pe.matmul(acc[r:r + 32, t // 4, 0:C + 1], lk[:, t, :], wt[:, t, :], start=True, stop=True)
            ins.then_inc(setup_g, 1)
            pe.wait_ge(setup_brow, 1)
            pe.matmul(prod[:, 3, 0:KV], ones, brow, start=True, stop=True).then_inc(setup_w, 1)
            pe.wait_ge(setup_rows, 1)
            pe.matmul(small[:, 0:4], mask, gl_max[:, :], start=True, stop=True).then_inc(setup_scale, 1)
            pe.wait_ge(setup_done, 1)

            def keep_clock(n):
                for _ in range(n):
                    pe.matmul(unread[:, 0:KV], w_hi[:, 0, 0:P], w_hi[:, 0, :], start=True, stop=True)

            def mean_over_group(b):
                pe.wait_ge(chan_ready, 2 * b + 1)
                pe.matmul(small[:, 0:HALVES], avg, chan[:, :, 0], start=True, stop=True).then_inc(group_sum, 1)

            def square_over_group(b):
                pe.wait_ge(chan_ready, 2 * b + 2)
                pe.matmul(small[:, 0:HALVES], avg, dev[:, :], start=True, stop=True).then_inc(group_sum, 1)

            def accumulate(n, j, start, stop):
                pe.wait_ge(v_scaled, n + 1)
                for t in range(GT):
                    for g in range(2):
                        ins = pe.matmul(acc[:, g, 0:P],
                                        kv[:, j % 4, t, 8 * g:8 * g + 8, :],
                                        kv[:, j % 4, t, HEADS + 8 * g:HEADS + 8 * g + 8, :],
                                        start=start and t == 0, stop=stop and t == GT - 1,
                                        skip_group_check=True)
                ins.then_inc(kv_done, 1)

            def project_first(b):
                pe.wait_ge(hi_ready, 2 * ISTEPS * b + 1)
                for t in range(GT):
                    for a in range(HALVES):
                        hi = y_hi[:, 0, a, t * TILE:(t + 1) * TILE]
                        pe.matmul(prod[:, t, 0:KV], hi, w_hi[:, a, :], start=a == 0, stop=False)
                        pe.matmul(prod[:, t, 0:KV], hi, w_lo[:, a, :], start=False, stop=False)
                pe.wait_ge(split_ready, 2 * ISTEPS * b + 1)
                for t in range(GT):
                    for a in range(HALVES):
                        ins = pe.matmul(prod[:, t, 0:KV], y_lo[:, 0, a, t * TILE:(t + 1) * TILE], w_hi[:, a, :],
                                        start=False, stop=a == HALVES - 1)
                ins.then_inc(projected, 1)

            def project(n, j):
                for t in range(GT):
                    o = prod[:, 2 * (j % 2) + t, 0:KV]
                    tok = (j % SPQ) * GT * TILE + t * TILE
                    for a in range(HALVES):
                        hi = y_hi[:, j // SPQ, a, tok:tok + TILE]
                        lo = y_lo[:, j // SPQ, a, tok:tok + TILE]
                        pe.matmul(o, hi, w_hi[:, a, :], start=a == 0, stop=False)
                        pe.matmul(o, hi, w_lo[:, a, :], start=False, stop=False)
                        ins = pe.matmul(o, lo, w_hi[:, a, :], start=False, stop=a == HALVES - 1)
                ins.then_inc(projected, 1)

            def image(b, more):
                def body(k, first, last):
                    n0 = (b * BLOCKS + k) * STEPS
                    for j in range(STEPS):
                        if first and j < 2:
                            pe.wait_ge(added, GRANT + IU * b - 1 + j)
                        if first and j == 0:
                            project_first(b)
                            continue
                        pe.wait_ge(split_ready, 2 * ISTEPS * b + STEPS * k + j + 1)
                        if not (first and j < 2):
                            pe.wait_ge(biased, n0 + j - 1)
                        project(n0 + j, j)
                        if not (first and j < 3):
                            accumulate(n0 + j - 3, (j - 3) % STEPS, first and j == 3, False)
                    if last:
                        for j, idle in ((STEPS - 3, IDLE[0]), (STEPS - 2, IDLE[1]), (STEPS - 1, 0)):
                            keep_clock(idle)
                            accumulate(n0 + j, j, False, j == STEPS - 1)
                        keep_clock(IDLE[2])
                blocks(pe, body)

                pe.wait_ge(s_ready, b + 1)
                pe.wait_ge(biased, ISTEPS * (b + 1))
                for g in range(2):
                    pe.matmul(prod[:, g, 0:C + 1], s_mat[:, g, :], g_mat[:, g, :], start=True, stop=True)\
                      .then_inc(u_prod, 1)
                for g in range(2):
                    pe.wait_ge(u_ready, 2 * b + g + 1)
                    for a in range(HALVES):
                        ins = pe.matmul(prod[:, 2 + g, a * P:(a + 1) * P], u_mat[:, g, a * P:(a + 1) * P],
                                        l_mat[:, g, :], start=True, stop=True)
                    ins.then_inc(m_prod, 1)
                for g in range(2):
                    ins = pe.matmul(small[:, 8 + g:9 + g], l_mat[:, g, :], u_mat[:, g, C:C + 1], start=True, stop=True)
                ins.then_inc(m_prod, 1)

                def body_b(k, last):
                    for u in range(UNITS):
                        part, half = u // 2, u % 2
                        if u < 2:
                            pe.wait_ge(m_ready, 2 * b + u + 1)
                        pe.wait_ge(added, IU * b + UNITS * k + u + 1)
                        cols = slice(half * P, (half + 1) * P)
                        for p in range(QPP):
                            q = QPP * part + p
                            if half == 0:
                                pe.wait_ge(split_ready, ISTEPS * (2 * b + 1) + STEPS * k + SPQ * (q + 1))
                            o = prod[:, 2 * half + p, :]
                            for a in range(HALVES):
                                pe.matmul(o, m_hi[:, a, cols], y_hi[:, q, a, :], start=a == 0, stop=False)
                                pe.matmul(o, m_hi[:, a, cols], y_lo[:, q, a, :], start=False, stop=False)
                                ins = pe.matmul(o, m_lo[:, a, cols], y_hi[:, q, a, :], start=False,
                                                stop=a == HALVES - 1)
                                if more and last and u == UNITS - 1 and a == HALVES - 1:
                                    if p == 0:
                                        mean_over_group(b + 1)
                                    else:
                                        square_over_group(b + 1)
                            if half == 1 and p == 0:
                                ins.then_inc(half_read, 1)
                        ins.then_inc(mixed, 1)

                with pe.Fori(0, BLOCKS - 1) as k:
                    body_b(k, False)
                body_b(BLOCKS - 1, True)
                if more:
                    keep_clock(IDLE[3])

            mean_over_group(0)
            square_over_group(0)
            images(pe, image)


def _tables():
    import numpy as np
    q = np.zeros((D, J))
    for j in range(J):
        q[:j + 1, j] = 1.0 / np.sqrt((j + 1) * (j + 2))
        q[j + 1, j] = -(j + 1) / np.sqrt((j + 1) * (j + 2))
    t = np.zeros((P, C_WIDTH))
    for h in range(2):
        for kind in range(2):
            r = 48 * h + 16 * (1 + kind)
            t[r:r + D, C_HEL + 30 * kind + J * h:C_HEL + 30 * kind + J * (h + 1)] = q
        t[48 * h:48 * h + D, C_QG + 16 * h:C_QG + 16 * h + J] = q
        t[48 * h:48 * h + D, C_EG + 16 * h + J] = 1.0
    for h in range(8):
        s = slice(16 * h, 16 * h + 16)
        t[16 * h:16 * h + J, C_QL + 16 * h:C_QL + 16 * h + 16] = q.T
        t[16 * h + J, C_EL + 16 * h:C_EL + 16 * h + 16] = 1.0
        t[s, C_MASK + 16 * h:C_MASK + 16 * h + 16] = 1.0 / N
    for g in range(P // GROUP):
        t[GROUP * g:GROUP * (g + 1), C_AVG + GROUP * g:C_AVG + GROUP * (g + 1)] = 1.0 / GROUP
    return t.astype(np.float32)


_INS = ["x", "L0_conv_w_qkv", "L0_conv_b_qkv", "L0_conv_kln_w", "L0_conv_kln_b", "L0_conv_vln_w", "L0_conv_vln_b"]


def kernel(**inputs):
    import numpy as _np
    import concourse.bacc as _bacc
    from concourse import mybir as _mybir
    from concourse.bass_utils import run_bass_kernel_spmd as _run

    nc = _bacc.Bacc("TRN2", target_bir_lowering=False, num_devices=1)
    arrays, args = {}, []
    for name in _INS:
        a = _np.ascontiguousarray(inputs[name])
        arrays[f"in_{name}"] = a
        args.append(nc.dram_tensor(f"in_{name}", a.shape, _mybir.dt.from_np(a.dtype), kind="ExternalInput").ap())
    tables = _tables()
    arrays["in_tables"] = tables
    args.append(nc.dram_tensor("in_tables", tables.shape, fp32, kind="ExternalInput").ap())
    args.append(nc.dram_tensor("out_0", (B, C, H, W), fp32, kind="ExternalOutput").ap())
    build(nc, *args)
    r = _run(nc, [arrays], core_ids=[0])
    return r.results[0]["out_0"]
```
